# Optimizing a Trainium2 kernel written in Bass

```python
import numpy as np
import jax
import jax.numpy as jnp

def _softmax(x, axis=-1):
    return jax.nn.softmax(x, axis=axis)

def _gelu(x):
    return jax.nn.gelu(x, approximate=True)

def _silu(x):
    return jax.nn.silu(x)

def _sigmoid(x):
    return jax.nn.sigmoid(x)

def _layernorm(x, axis=-1, eps=1e-05):
    m = jnp.mean(x, axis=axis, keepdims=True)
    v = jnp.var(x, axis=axis, keepdims=True)
    return (x - m) / jnp.sqrt(v + eps)

def _scatter_add(tgt, idx, src, axis=0):
    return tgt.at[idx].add(src)

def _segment_sum(src, seg, n):
    return jax.ops.segment_sum(src, seg, n)
kernel_name = 'mk_cond_resid_d4_seqx_r8_e43b29'

def setup_inputs(seed: int=0):
    np.random.seed(seed)
    _w = jnp.asarray

    def _rec_inputs():
        import jax
        import jax.numpy as jnp
        _rk = jax.random.key(seed)
        x = -7.109e-05 + 0.9999 * jax.random.normal(jax.random.fold_in(_rk, 1), (64, 32, 512), jnp.float32)
        _lenS = 32 - jax.random.randint(jax.random.fold_in(_rk, 7), (64,), 0, max(1, 32 // 4) + 1, jnp.int32)
        _lenS2 = 32 - jax.random.randint(jax.random.fold_in(_rk, 8), (64,), 0, max(1, 32 // 4) + 1, jnp.int32)
        itok_B_0_15 = jax.random.randint(jax.random.fold_in(_rk, 11), (64,), 0, 16, jnp.int32)
        itok_B_0_7 = jax.random.randint(jax.random.fold_in(_rk, 12), (64,), 0, 8, jnp.int32)
        itok_Bx16_0_63 = jax.random.randint(jax.random.fold_in(_rk, 13), (64, 16), 0, 64, jnp.int32)
        itok_B_207_1644 = jax.random.randint(jax.random.fold_in(_rk, 14), (64,), 207, 1645, jnp.int32)
        return (x, itok_B_0_15, itok_B_0_7, itok_Bx16_0_63, itok_B_207_1644)
    x, itok_B_0_15, itok_B_0_7, itok_Bx16_0_63, itok_B_207_1644 = _rec_inputs()

    def _L0_cond_setup():
        import jax, jax.numpy as jnp
        import numpy as np
        B, C, T = (64, 32, 512)
        S, D = (16, 32)
        key = jax.random.key(seed)
        k1, k2, k3 = jax.random.split(key, 3)
        x = jax.random.normal(k1, (B, C, T), dtype=jnp.float32)
        condition = jax.random.randint(k2, (B,), 0, S, dtype=jnp.int64)
        bound = float(np.sqrt(6.0 / C))
        weights = jax.random.uniform(k3, (S, C, D), dtype=jnp.float32, minval=-bound, maxval=bound)
        return {'x': x, 'condition': condition, 'weights': weights}
    _L0_cond_all = _L0_cond_setup()
    _L0_cond_in = {k: v for k, v in _L0_cond_all.items() if k in ('weights',)}
    del _L0_cond_all

    def _L1_cond_setup():
        import jax, jax.numpy as jnp
        import numpy as np
        TOP_K = 2
        LANG_BIAS = 5.0
        SCALING = 32.0 / 16.0
        LANGUAGE_PAD_ID = -1
        key = jax.random.key(seed)
        ks = jax.random.split(key, 6)
        B, T, D, O, E, R = (4, 256, 512, 512, 8, 16)
        x = jax.random.normal(ks[0], (B, T, D), dtype=jnp.float32)
        language_ids = jax.random.randint(ks[1], (B,), 0, E).astype(jnp.int64)
        W = jax.random.normal(ks[2], (O, D), dtype=jnp.float32) * (1.0 / np.sqrt(D))
        Wr = jax.random.normal(ks[3], (E, D), dtype=jnp.float32) * (1.0 / np.sqrt(D))
        A = jax.random.normal(ks[4], (E, R, D), dtype=jnp.float32) * (1.0 / np.sqrt(D))
        Bm = jax.random.normal(ks[5], (O, R), dtype=jnp.float32) * 0.0
        Bm = jnp.broadcast_to(Bm, (E, O, R)) + jax.random.normal(ks[5], (E, O, R), dtype=jnp.float32) * 0.02
        return {'x': x, 'language_ids': language_ids, 'W': W, 'Wr': Wr, 'A': A, 'B': Bm}
    _L1_cond_all = _L1_cond_setup()
    _L1_cond_in = {k: v for k, v in _L1_cond_all.items() if k in ('W', 'Wr', 'A', 'B')}
    del _L1_cond_all

    def _L2_cond_setup():
        import jax, jax.numpy as jnp
        import numpy as np
        NUM_CONDITIONS = 16
        IN_CH = 32
        OUT_CH = 32
        B = 64
        T = 512
        key = jax.random.key(seed)
        k_x, k_w, k_c = jax.random.split(key, 3)
        x = jax.random.normal(k_x, (B, IN_CH, T), dtype=jnp.float32)
        bound = float(np.sqrt(6.0 / IN_CH))
        weights = jax.random.uniform(k_w, (NUM_CONDITIONS, IN_CH, OUT_CH), dtype=jnp.float32, minval=-bound, maxval=bound)
        condition = jax.random.randint(k_c, (B,), 0, NUM_CONDITIONS, dtype=jnp.int64)
        return {'x': x, 'weights': weights, 'condition': condition}
    _L2_cond_all = _L2_cond_setup()
    _L2_cond_in = {k: v for k, v in _L2_cond_all.items() if k in ('weights',)}
    del _L2_cond_all

    def _L3_cond_setup():
        import jax, jax.numpy as jnp
        import numpy as np
        B, S, HID = (4, 128, 512)
        D, HQ, HK = (128, 32, 8)
        PAGES, PSIZE, NPP = (64, 32, 16)
        THETA = 10000.0
        EPS = 1e-06
        SCALE = 1.0 / float(np.sqrt(D))

        def _rmsnorm(t, w):
            var = jnp.mean(t * t, axis=-1, keepdims=True)
            return t * jax.lax.rsqrt(var + EPS) * w

        def _rope(t, pos):
            inv_freq = 1.0 / THETA ** (jnp.arange(0, D, 2, dtype=jnp.float32) / D)
            freqs = pos[..., None].astype(jnp.float32) * inv_freq
            cos = jnp.cos(freqs)[:, :, None, :]
            sin = jnp.sin(freqs)[:, :, None, :]
            t1, t2 = (t[..., :D // 2], t[..., D // 2:])
            return jnp.concatenate([t1 * cos - t2 * sin, t2 * cos + t1 * sin], axis=-1)
        key = jax.random.key(seed)
        ks = jax.random.split(key, 10)
        x = jax.random.normal(ks[0], (B, S, HID), jnp.float32)
        Wq = jax.random.normal(ks[1], (HQ * D, HID), jnp.float32) * 0.02
        Wk = jax.random.normal(ks[2], (HK * D, HID), jnp.float32) * 0.02
        Wv = jax.random.normal(ks[3], (HK * D, HID), jnp.float32) * 0.02
        Wo = jax.random.normal(ks[4], (HID, HQ * D), jnp.float32) * 0.02
        q_norm_w = jax.random.uniform(ks[5], (D,), jnp.float32)
        k_norm_w = jax.random.uniform(ks[6], (D,), jnp.float32)
        k_cache = jax.random.normal(ks[7], (PAGES, PSIZE, HK, D), jnp.float32)
        v_cache = jax.random.normal(ks[8], (PAGES, PSIZE, HK, D), jnp.float32)
        block_table = jnp.arange(B * NPP, dtype=jnp.int32).reshape(B, NPP)
        cache_seqlens = jax.random.randint(ks[9], (B,), 0, 475).astype(jnp.int32)
        return dict(x=x, Wq=Wq, Wk=Wk, Wv=Wv, Wo=Wo, q_norm_w=q_norm_w, k_norm_w=k_norm_w, k_cache=k_cache, v_cache=v_cache, block_table=block_table, cache_seqlens=cache_seqlens)
    _L3_cond_all = _L3_cond_setup()
    _L3_cond_in = {k: v for k, v in _L3_cond_all.items() if k in ('Wq', 'Wk', 'Wv', 'Wo', 'q_norm_w', 'k_norm_w', 'k_cache', 'v_cache')}
    del _L3_cond_all
    return {'x': x, 'itok_B_0_15': itok_B_0_15, 'itok_B_0_7': itok_B_0_7, 'itok_Bx16_0_63': itok_Bx16_0_63, 'itok_B_207_1644': itok_B_207_1644, 'L0_cond_weights': _L0_cond_in['weights'], 'L1_cond_W': _L1_cond_in['W'], 'L1_cond_Wr': _L1_cond_in['Wr'], 'L1_cond_A': _L1_cond_in['A'], 'L1_cond_B': _L1_cond_in['B'], 'L2_cond_weights': _L2_cond_in['weights'], 'L3_cond_Wq': _L3_cond_in['Wq'], 'L3_cond_Wk': _L3_cond_in['Wk'], 'L3_cond_Wv': _L3_cond_in['Wv'], 'L3_cond_Wo': _L3_cond_in['Wo'], 'L3_cond_q_norm_w': _L3_cond_in['q_norm_w'], 'L3_cond_k_norm_w': _L3_cond_in['k_norm_w'], 'L3_cond_k_cache': _L3_cond_in['k_cache'], 'L3_cond_v_cache': _L3_cond_in['v_cache']}

def reference(x, itok_B_0_15, itok_B_0_7, itok_Bx16_0_63, itok_B_207_1644, L0_cond_weights, L1_cond_W, L1_cond_Wr, L1_cond_A, L1_cond_B, L2_cond_weights, L3_cond_Wq, L3_cond_Wk, L3_cond_Wv, L3_cond_Wo, L3_cond_q_norm_w, L3_cond_k_norm_w, L3_cond_k_cache, L3_cond_v_cache):
    import jax
    import jax.numpy as jnp

    def _L0_cond_ref(x, condition, weights):
        import jax, jax.numpy as jnp
        import numpy as np
        B, C, T = (64, 32, 512)
        S, D = (16, 32)
        W = weights[condition]
        return jnp.einsum('bct,bcd->bdt', x, W)

    def _L1_cond_ref(x, language_ids, W, Wr, A, B):
        import jax, jax.numpy as jnp
        import numpy as np
        TOP_K = 2
        LANG_BIAS = 5.0
        SCALING = 32.0 / 16.0
        LANGUAGE_PAD_ID = -1
        base = jnp.einsum('btd,od->bto', x, W)
        E = Wr.shape[0]
        logits = jnp.einsum('btd,ed->bte', x.astype(jnp.float32), Wr.astype(jnp.float32))
        expert_targets = language_ids
        valid = expert_targets >= 0
        tgt = jnp.where(valid, expert_targets, 0)
        bias = jax.nn.one_hot(tgt, E, dtype=logits.dtype) * LANG_BIAS
        bias = jnp.where(valid[:, None], bias, 0.0)
        logits = logits + bias[:, None, :]
        topw, topi = jax.lax.top_k(logits, TOP_K)
        weights = jax.nn.softmax(topw, axis=-1)
        gates = jnp.sum(jax.nn.one_hot(topi, E, dtype=weights.dtype) * weights[..., None], axis=-2)
        gates = gates.astype(x.dtype)
        h = jnp.einsum('btd,erd->bter', x, A)
        lora_out = jnp.einsum('bter,bte,eor->bto', h, gates, B)
        return base + SCALING * lora_out

    def _L2_cond_ref(x, weights, condition):
        import jax, jax.numpy as jnp
        import numpy as np
        NUM_CONDITIONS = 16
        IN_CH = 32
        OUT_CH = 32
        B = 64
        T = 512
        W = weights[condition]
        return jnp.einsum('bct,bcd->bdt', x, W)

    def _L3_cond_ref(x, Wq, Wk, Wv, Wo, q_norm_w, k_norm_w, k_cache, v_cache, block_table, cache_seqlens):
        import jax, jax.numpy as jnp
        import numpy as np
        B, S, HID = (4, 128, 512)
        D, HQ, HK = (128, 32, 8)
        PAGES, PSIZE, NPP = (64, 32, 16)
        THETA = 10000.0
        EPS = 1e-06
        SCALE = 1.0 / float(np.sqrt(D))

        def _rmsnorm(t, w):
            var = jnp.mean(t * t, axis=-1, keepdims=True)
            return t * jax.lax.rsqrt(var + EPS) * w

        def _rope(t, pos):
            inv_freq = 1.0 / THETA ** (jnp.arange(0, D, 2, dtype=jnp.float32) / D)
            freqs = pos[..., None].astype(jnp.float32) * inv_freq
            cos = jnp.cos(freqs)[:, :, None, :]
            sin = jnp.sin(freqs)[:, :, None, :]
            t1, t2 = (t[..., :D // 2], t[..., D // 2:])
            return jnp.concatenate([t1 * cos - t2 * sin, t2 * cos + t1 * sin], axis=-1)
        bsz, seqlen, _ = x.shape
        q = jnp.einsum('bsd,ed->bse', x, Wq).reshape(bsz, seqlen, HQ, D)
        k = jnp.einsum('bsd,ed->bse', x, Wk).reshape(bsz, seqlen, HK, D)
        v = jnp.einsum('bsd,ed->bse', x, Wv).reshape(bsz, seqlen, HK, D)
        q = _rmsnorm(q, q_norm_w)
        k = _rmsnorm(k, k_norm_w)
        pos = cache_seqlens[:, None] + jnp.arange(seqlen)[None, :]
        q = _rope(q, pos)
        k = _rope(k, pos)
        L = NPP * PSIZE
        kc = k_cache[block_table].reshape(bsz, L, HK, D)
        vc = v_cache[block_table].reshape(bsz, L, HK, D)
        k_all = jnp.concatenate([kc, k], axis=1)
        v_all = jnp.concatenate([vc, v], axis=1)
        valid_c = jnp.arange(L)[None, :] < cache_seqlens[:, None]
        valid = jnp.concatenate([valid_c, jnp.ones((bsz, seqlen), dtype=bool)], axis=1)
        rep = HQ // HK
        k_all = jnp.repeat(k_all, rep, axis=2)
        v_all = jnp.repeat(v_all, rep, axis=2)
        scores = jnp.einsum('bqhd,bkhd->bhqk', q, k_all) * SCALE
        scores = jnp.where(valid[:, None, None, :], scores, -1e+30)
        probs = jax.nn.softmax(scores, axis=-1)
        o = jnp.einsum('bhqk,bkhd->bqhd', probs, v_all)
        o = o.reshape(bsz, seqlen, HQ * D)
        return jnp.einsum('bse,de->bsd', o, Wo)
    x = x + _L0_cond_ref(x, itok_B_0_15, L0_cond_weights)
    x = x + _L1_cond_ref(x, itok_B_0_7, L1_cond_W, L1_cond_Wr, L1_cond_A, L1_cond_B)
    x = x + _L2_cond_ref(x, L2_cond_weights, itok_B_0_15)
    x = x + _L3_cond_ref(x, L3_cond_Wq, L3_cond_Wk, L3_cond_Wv, L3_cond_Wo, L3_cond_q_norm_w, L3_cond_k_norm_w, L3_cond_k_cache, L3_cond_v_cache, itok_Bx16_0_63, itok_B_207_1644)
    return x

_drawn_inputs = setup_inputs


def setup_inputs(seed=0):
    import zlib

    import numpy as np

    out = dict(_drawn_inputs(seed))
    spreads = {}
    factors = {'L3_cond_Wq': 5.725,
     'L3_cond_Wk': 8.0,
     'L3_cond_Wv': 8.0,
     'L3_cond_Wo': 3.103,
     'L3_cond_q_norm_w': 8.0,
     'L3_cond_k_norm_w': 8.0,
     'L3_cond_k_cache': 6.03,
     'L3_cond_v_cache': 3.306}
    for name, (base, spread) in spreads.items():
        noise = np.random.default_rng([zlib.crc32(name.encode()), seed]).standard_normal(out[name].shape)
        drawn = base * np.exp(spread * noise) if base else spread * noise
        out[name] = jnp.asarray(drawn.astype(out[name].dtype))
    for name, factor in factors.items():
        out[name] = (out[name] * factor).astype(out[name].dtype)
    return out
```

```python
from contextlib import ExitStack

import concourse.bass as bass
from concourse import mybir
from concourse.alu_op_type import AluOpType as ALU

F32, F16, BF16 = mybir.dt.float32, mybir.dt.float16, mybir.dt.bfloat16
I32, U32 = mybir.dt.int32, mybir.dt.uint32
ACT = mybir.ActivationFunctionType
AX = mybir.AxisListType
SP = mybir.EngineType.SP
RMAX = bass.bass_isa.ReduceOp.max
ds = bass.ds

P = 128
B, S, D = 64, 32, 512
BT = P // S
NT = B // BT
KD = D // P
SETS, MIX = 16, 32
E, R = 8, 16
ER = E * R
ROUTE = E + ER
HD, HQ, HK = 128, 32, 8
REP = HQ // HK
PAGES, PS, NPP = 64, 32, 16
L = PS * NPP
LK = L + S
LC = L // P
NQ, NKV = HQ * HD, HK * HD
NW = NQ + 2 * NKV
QB, KB, VB = NQ // D, NKV // D, NKV // D
ROT = QB + KB
BLK = ROT + VB
HB = D // HD
HALF = HD // 2
HALVES = ROT * HB
PG = HK * 2 * PS
EPS = 1e-6
SCALE = float(HD) ** -0.5
TOP = 2.0 ** 14
TINY = 2.0 ** -16
EXPONENT = 0x7F800000
MASKED = -1e30
LANG_BIAS, LORA = 5.0, 32.0 / 16.0
ROUND = 1.5 * 2.0 ** 23
TWO_PI = (6.28125, 0.0019350051879882812, 3.019916050561733e-07)
CH = 4096
SC = 1024


def after(eng, sem, value):
    if not isinstance(value, int) or value > 0:
        eng.wait_ge(sem, value)


def hold(eng, sem, value, passed):
    eng.wait_ge(sem, value)
    eng.sem_inc(passed, 1)


def conditional_residual(nc, x, cond_r, lang_r, len_r, lens, pages, pages_r, mix0, mix2, lin_t, router_t, a_t,
                         b_t, wq_t, wk_t, wv_t, wo_t, q_norm, k_norm, k_t, v_rows, inv_freq, out):
    x_v = x.rearrange("(t b) s d -> t (b s) d", b=BT)
    out_v = out.rearrange("(t b) s d -> t (b s) d", b=BT)
    x3_d = nc.dram_tensor("x3_scratch", (NT, P, D), F32).ap()
    k_d = nc.dram_tensor("k_parts", (PAGES, P, PG), F16).ap()
    v_d = nc.dram_tensor("v_parts", (PAGES * PS, HK * 2 * HD), F16).ap()
    wo_d = nc.dram_tensor("wo_parts", (P, HQ, 2, D), F16).ap()
    kn_d = nc.dram_tensor("k_new_parts", (B, P, PG), F16).ap()
    vn_d = nc.dram_tensor("v_new_parts", (B, P, NKV), BF16).ap()
    q_d = nc.dram_tensor("q_parts", (NT, QB, P, BT, 2 * HB * S), F16).ap()

    whole = ExitStack()
    with whole:
        def keep(name, shape, dt):
            return whole.enter_context(nc.sbuf_tensor(name, shape, dt))

        ident = keep("ident", [P, P], F32)
        ident16 = keep("ident16", [P, P], F16)
        mag = keep("mag", [P, 5], F32)
        pow2 = keep("pow2", [P, 5], F32)
        up = keep("up", [P, 5], F32)
        down = keep("down", [P, 5], F32)
        cs = keep("cs", [P, 2], F32)
        vw = keep("vw", [P, 1], F32)
        oscale = keep("oscale", [P, 1], F32)
        v_idx = keep("v_idx", [P, B * LC], I32)
        lens_f = keep("lens_f", [P, B], F32)
        page_row = keep("page_row", [1, B * NPP], I32)

        ab = ExitStack()
        with ab:
            def mid(name, shape, dt):
                return ab.enter_context(nc.sbuf_tensor(name, shape, dt))

            cos = mid("cos", [P, NT, HALF], F32)
            sin = mid("sin", [P, NT, HALF], F32)
            wa = mid("wa", [P, 2, HD], F32)
            wb = mid("wb", [P, 2, HD], F32)
            parts = (ident, ident16, mag, pow2, up, down, cs, vw, oscale, v_idx, lens_f, page_row)
            with ExitStack() as mix:
                mt = lambda name, shape, dt: mix.enter_context(nc.sbuf_tensor(name, shape, dt))
                blocks = mt("blocks", [P, BT, S], F32)
                g0 = mt("g0", [P, NT, MIX], F32)
                g2 = mt("g2", [P, NT, MIX], F32)
                bias = mt("bias", [P, NT, E], F32)
                iota8 = mt("iota8", [P, E], F32)
                prologue(nc, parts, cos, sin, wa, wb, blocks, g0, g2, bias, iota8, cond_r, lang_r, len_r, lens,
                         pages, pages_r, mix0, mix2, wq_t, wk_t, wv_t, wo_t, q_norm, k_norm, k_t, v_rows,
                         inv_freq)
                mixing(nc, ident, blocks, g0, g2, bias, iota8, x_v, lin_t, router_t, a_t, b_t, x3_d)
            wh = mid("wh", [P, KD, NW], F16)
            wl = mid("wl", [P, KD, NW], F16)
            splitting(nc, up, wh, wl, wq_t, wk_t, wv_t, wo_t, k_t, v_rows, k_d, v_d, wo_d)
            projections(nc, ident, ident16, up, down, vw, cos, sin, wa, wb, wh, wl, x3_d, q_d, kn_d, vn_d)
        attention(nc, ident, cs, oscale, v_idx, lens_f, page_row, k_d, v_d, kn_d, vn_d, q_d, wo_d, x3_d, out_v)


def prologue(nc, parts, cos, sin, wa, wb, blocks, g0, g2, bias, iota8, cond_r, lang_r, len_r, lens, pages,
             pages_r, mix0, mix2, wq_t, wk_t, wv_t, wo_t, q_norm, k_norm, k_t, v_rows, inv_freq):
    (ident, ident16, mag, pow2, up, down, cs, vw, oscale, v_idx, lens_f, page_row) = parts
    k_c = k_t.rearrange("(c n) p m -> c p n m", n=CH // (HK * PS))
    v_c = v_rows.rearrange("(c n p) m -> c p n m", p=P, n=CH // NKV)
    wo_c = wo_t.rearrange("(c n p) m -> c p n m", p=P, n=CH // D)
    q_c = wq_t.rearrange("(c p) m -> c p m", p=P)
    kk_c = wk_t.rearrange("(n p) m -> p n m", p=P)
    vv_c = wv_t.rearrange("(n p) m -> p n m", p=P)
    ctx = ExitStack()
    with ctx:
        def sb(name, shape, dt):
            return ctx.enter_context(nc.sbuf_tensor("pro_" + name, shape, dt))

        def sem(name):
            return ctx.enter_context(nc.semaphore("pro_" + name))

        NBUF = 4
        ring = sb("ring", [P, NBUF, CH], F32)
        found = sb("found", [P, 18], F32)
        cond_i = sb("cond_i", [P, NT], I32)
        lang_i = sb("lang_i", [P, NT], I32)
        len_i = sb("len_i", [P, NT], I32)
        lens_i = sb("lens_i", [P, B], I32)
        small = sb("small", [P, 4, NT], F32)
        row_i = sb("row_i", [P, 1], I32)
        row_f = sb("row_f", [P, 1], F32)
        mix_idx = sb("mix_idx", [P, NT], U32)
        mix_col = sb("mix_col", [P, NT], F32)
        pages_i = sb("pages_i", [P, B * LC], I32)
        pages_f = sb("pages_f", [P, B * LC], F32)
        iota_i = sb("iota_i", [P, E], I32)
        norms = sb("norms", [P, 2, HD], F32)
        freq = sb("freq", [P, HALF], F32)
        angle = sb("angle", [P, NT, HALF], F32)
        turns = sb("turns", [P, NT, HALF], F32)
        fold = sb("fold", [P, NT, HALF], F32)

        loaded = [sem(f"loaded{i}") for i in range(NBUF)]
        scanned, inputs, made, gathered = sem("scanned"), sem("inputs"), sem("made"), sem("gathered")
        chain, reduced, ready, local = sem("chain"), sem("reduced"), sem("index_ready"), sem("local")
        trig, tables, pool_chain = sem("trig"), sem("tables"), sem("pool_chain")

        sources = ([(0, k_c[c]) for c in range(4)] + [(1, v_c[c]) for c in range(4)]
                   + [(2, wo_c[c]) for c in range(4)] + [(3, q_c[c]) for c in range(4)]
                   + [(3, kk_c), (3, vv_c)])
        block = ctx.enter_context(nc.Block())
        N_IN = 4 * 4 + 1 + 1 + 2 + 1

        @block.sync
        def _(sp):
            for r in range(BT):
                rows = slice(r * S, (r + 1) * S)
                for dst, src in ((cond_i, cond_r), (lang_i, lang_r), (len_i, len_r), (pages_i, pages_r)):
                    sp.dma_start(dst[rows, :], src[r:r + 1, :].to_broadcast([S, src.shape[1]])).then_inc(inputs, 16)
            sp.dma_start(lens_i[:, :], lens.rearrange("(o b) -> o b", o=1).to_broadcast([P, B])).then_inc(inputs, 16)
            sp.dma_start(page_row[:, :], pages.rearrange("(o b) j -> o (b j)", o=1)).then_inc(inputs, 16)
            for i, w in enumerate((q_norm, k_norm)):
                sp.dma_start(norms[:, i, :], w.rearrange("(o d) -> o d", o=1).to_broadcast([P, HD])).then_inc(inputs, 16)
            sp.dma_start(freq[:, :], inv_freq.rearrange("(o d) -> o d", o=1).to_broadcast([P, HALF])).then_inc(inputs, 16)
            for i, (_, src) in enumerate(sources):
                after(sp, scanned, i - NBUF + 1)
                dst = ring[:, i % NBUF, :]
                if len(src.shape) == 3:
                    dst = dst.rearrange("p (n m) -> p n m", m=src.shape[2])
                sp.dma_start(dst, src).then_inc(loaded[i % NBUF], 16)

        @block.gpsimd
        def _(pool):
            n = 0

            def step(ins):
                nonlocal n
                n += 1
                ins.then_inc(pool_chain, 1)
                pool.wait_ge(pool_chain, n)

            step(nc.gpsimd.memset(ident[:, :], 0.0))
            step(nc.gpsimd.affine_select(out=ident[:, :], in_=ident[:, :], compare_op=ALU.not_equal, fill=1.0,
                                         base=0, pattern=[[-1, P]], channel_multiplier=1))
            step(nc.gpsimd.tensor_copy(ident16[:, :], ident[:, :]))
            step(nc.gpsimd.memset(blocks[:, :, :], 1.0))
            step(nc.gpsimd.affine_select(out=blocks[:, :, :], in_=blocks[:, :, :], compare_op=ALU.is_ge, fill=0.0,
                                         base=0, pattern=[[-S, BT], [0, S]], channel_multiplier=1))
            step(nc.gpsimd.affine_select(out=blocks[:, :, :], in_=blocks[:, :, :], compare_op=ALU.is_ge, fill=0.0,
                                         base=S - 1, pattern=[[S, BT], [0, S]], channel_multiplier=-1))
            step(nc.gpsimd.iota(iota_i[:, :], pattern=[[1, E]], base=0, channel_multiplier=0))
            step(nc.gpsimd.tensor_copy(iota8[:, :], iota_i[:, :]))
            step(nc.gpsimd.iota(row_i[:, :], pattern=[[0, 1]], base=0, channel_multiplier=1))
            nc.gpsimd.tensor_copy(row_f[:, :], row_i[:, :]).then_inc(made, 1)
            pool.wait_ge(ready, 1)
            for t in range(NT):
                for dst, src in ((g0, mix0), (g2, mix2)):
                    nc.gpsimd.indirect_dma_start(out=dst[:, t, :], out_offset=None, in_=src,
                                                 in_offset=bass.IndirectOffsetOnAxis(mix_idx[:, t:t + 1], 0)
                                                 ).then_inc(gathered, 16)
            pool.wait_ge(local, 1)
            nc.gpsimd.partition_all_reduce(mag[:, 0:4], pow2[:, 0:4], P, RMAX).then_inc(reduced, 1)
            pool.wait_ge(gathered, 2 * NT * 16)

        @block.vector
        def _(dve):
            n = 0

            def step(ins):
                nonlocal n
                n += 1
                ins.then_inc(chain, 1)
                dve.wait_ge(chain, n)

            v = nc.vector
            dve.wait_ge(inputs, N_IN * 16)
            dve.wait_ge(made, 1)
            step(v.tensor_copy(small[:, 0, :], cond_i[:, :]))
            step(v.tensor_copy(small[:, 1, :], len_i[:, :]))
            step(v.tensor_copy(small[:, 2, :], lang_i[:, :]))
            step(v.tensor_copy(lens_f[:, :], lens_i[:, :]))
            step(v.tensor_copy(pages_f[:, :], pages_i[:, :]))
            step(v.tensor_scalar(out=small[:, 3, 0:1], in0=row_f[:, :], scalar1=float(S), scalar2=-float(S),
                                 op0=ALU.is_ge, op1=ALU.mult))
            for r in range(2, BT):
                step(v.tensor_scalar(out=small[:, 3, r:r + 1], in0=row_f[:, :], scalar1=float(r * S),
                                     scalar2=-float(S), op0=ALU.is_ge, op1=ALU.mult))
                step(v.tensor_tensor(small[:, 3, 0:1], small[:, 3, 0:1], small[:, 3, r:r + 1], ALU.add))
            step(v.tensor_tensor(small[:, 3, 1:2], small[:, 3, 0:1], row_f[:, :], ALU.add))
            within = small[:, 3, 1:2]
            step(v.tensor_scalar(out=mix_col[:, :], in0=small[:, 0, :], scalar1=float(MIX), scalar2=within,
                                 op0=ALU.mult, op1=ALU.add))
            v.tensor_copy(mix_idx[:, :], mix_col[:, :]).then_inc(ready, 1)
            step(v.tensor_scalar(out=pages_f[:, :], in0=pages_f[:, :], scalar1=float(PS), scalar2=within,
                                 op0=ALU.mult, op1=ALU.add))
            step(v.tensor_copy(v_idx[:, :], pages_f[:, :]))
            for t in range(NT):
                last = v.tensor_scalar(out=bias[:, t, :], in0=iota8[:, :], scalar1=small[:, 2, t:t + 1],
                                       scalar2=LANG_BIAS, op0=ALU.is_equal, op1=ALU.mult)
            step(last)
            step(v.tensor_scalar(out=small[:, 1, :], in0=small[:, 1, :], scalar1=within, scalar2=None, op0=ALU.add))
            step(v.tensor_tensor(angle[:, :, :], small[:, 1, :].unsqueeze(2).to_broadcast([P, NT, HALF]),
                                 freq[:, :].unsqueeze(1).to_broadcast([P, NT, HALF]), ALU.mult))
            step(v.tensor_scalar(out=turns[:, :, :], in0=angle[:, :, :], scalar1=1.0 / 6.283185307179586,
                                 scalar2=ROUND, op0=ALU.mult, op1=ALU.add))
            step(v.tensor_scalar(out=turns[:, :, :], in0=turns[:, :, :], scalar1=-ROUND, scalar2=None, op0=ALU.add))
            for part in TWO_PI:
                step(v.scalar_tensor_tensor(out=angle[:, :, :], in0=turns[:, :, :], scalar=-part,
                                            in1=angle[:, :, :], op0=ALU.mult, op1=ALU.add))
            step(v.tensor_scalar(out=angle[:, :, :], in0=angle[:, :, :], scalar1=3.1415925, scalar2=-3.1415925,
                                 op0=ALU.min, op1=ALU.max))
            step(v.tensor_scalar(out=fold[:, :, :], in0=angle[:, :, :], scalar1=-1.0, scalar2=None, op0=ALU.mult))
            step(v.tensor_tensor(fold[:, :, :], fold[:, :, :], angle[:, :, :], ALU.min))
            v.tensor_scalar(out=fold[:, :, :], in0=fold[:, :, :], scalar1=1.5707963267948966, scalar2=None,
                            op0=ALU.add).then_inc(trig, 1)
            for i in range(len(sources)):
                dve.wait_ge(loaded[i % NBUF], 16 * (i // NBUF + 1))
                v.tensor_reduce(found[:, i:i + 1], ring[:, i % NBUF, :], AX.X, ALU.max,
                                apply_absolute_value=True).then_inc(scanned, 1)
            dve.wait_ge(scanned, len(sources))
            for col in range(4):
                mine = [i for i, (c, _) in enumerate(sources) if c == col]
                step(v.tensor_reduce(pow2[:, col:col + 1], found[:, mine[0]:mine[-1] + 1], AX.X, ALU.max))
            step(v.tensor_reduce(pow2[:, 4:5], norms[:, 0, :], AX.X, ALU.max, apply_absolute_value=True))
            step(v.tensor_reduce(up[:, 0:1], norms[:, 1, :], AX.X, ALU.max, apply_absolute_value=True))
            step(v.tensor_scalar(out=mag[:, 4:5], in0=pow2[:, 4:5], scalar1=16.0, scalar2=None, op0=ALU.mult))
            step(v.tensor_scalar(out=up[:, 0:1], in0=up[:, 0:1], scalar1=16.0, scalar2=None, op0=ALU.mult))
            v.tensor_tensor(pow2[:, 0:1], pow2[:, 0:1], up[:, 0:1], ALU.max).then_inc(local, 1)
            dve.wait_ge(reduced, 1)
            step(v.tensor_scalar(out=mag[:, :], in0=mag[:, :], scalar1=TINY, scalar2=None, op0=ALU.max))
            step(v.tensor_scalar(out=pow2[:, :].bitcast(I32), in0=mag[:, :].bitcast(I32), scalar1=EXPONENT,
                                 scalar2=None, op0=ALU.bitwise_and))
            step(v.reciprocal(up[:, :], pow2[:, :]))
            step(v.tensor_scalar(out=up[:, :], in0=up[:, :], scalar1=TOP, scalar2=None, op0=ALU.mult))
            step(v.tensor_scalar(out=down[:, :], in0=pow2[:, :], scalar1=1.0 / TOP, scalar2=None, op0=ALU.mult))
            step(v.tensor_tensor(cs[:, 0:1], down[:, 0:1], down[:, 4:5], ALU.mult))
            step(v.tensor_scalar(out=cs[:, 0:1], in0=cs[:, 0:1], scalar1=SCALE, scalar2=None, op0=ALU.mult))
            step(v.tensor_scalar(out=cs[:, 1:2], in0=cs[:, 0:1], scalar1=-1.0, scalar2=None, op0=ALU.mult))
            step(v.tensor_tensor(vw[:, :], up[:, 1:2], down[:, 3:4], ALU.mult))
            step(v.tensor_tensor(oscale[:, :], down[:, 1:2], down[:, 2:3], ALU.mult))
            for i, col in enumerate((4, 0)):
                step(v.tensor_scalar(out=wa[:, i, :], in0=norms[:, i, :], scalar1=up[:, col:col + 1], scalar2=None,
                                     op0=ALU.mult))
                step(v.tensor_scalar(out=wb[:, i, 0:HALF], in0=wa[:, i, HALF:HD], scalar1=-1.0, scalar2=None,
                                     op0=ALU.mult))
                step(v.tensor_copy(wb[:, i, HALF:HD], wa[:, i, 0:HALF]))

        @block.scalar
        def _(act):
            act.wait_ge(trig, 1)
            nc.scalar.activation(sin[:, :, :], angle[:, :, :], ACT.Sin)
            nc.scalar.activation(cos[:, :, :], fold[:, :, :], ACT.Sin).then_inc(tables, 1)
            act.wait_ge(tables, 1)


def mixing(nc, ident, blocks, g0, g2, bias, iota8, x_v, lin_t, router_t, a_t, b_t, x3_d):
    TI = 4
    ctx = ExitStack()
    with ctx:
        def sb(name, shape, dt):
            return ctx.enter_context(nc.sbuf_tensor("mix_" + name, shape, dt))

        def sem(name):
            return ctx.enter_context(nc.semaphore("mix_" + name))

        lin = sb("lin", [P, KD, D], F32)
        route = sb("route", [P, KD, ROUTE], F32)
        low = sb("low", [ER, D], F32)
        xa = [sb(f"xa{j}", [P, D], F32) for j in range(TI)]
        xb = [sb(f"xb{j}", [P, D], F32) for j in range(TI)]
        xc = [sb(f"xc{j}", [P, D], F32) for j in range(TI)]
        xd = [sb(f"xd{j}", [P, D], F32) for j in range(TI)]
        m0 = [sb(f"m0{j}", [P, BT, MIX], F32) for j in range(TI)]
        m2 = [sb(f"m2{j}", [P, BT, MIX], F32) for j in range(TI)]
        x1t = [sb(f"x1t{j}", [P, D], F32) for j in range(TI)]
        logit = [sb(f"logit{j}", [P, E], F32) for j in range(TI)]
        top = [sb(f"top{j}", [P, 8], F32) for j in range(TI)]
        top_i = [sb(f"top_i{j}", [P, 8], U32) for j in range(TI)]
        top_f = [sb(f"top_f{j}", [P, 8], F32) for j in range(TI)]
        gate = [sb(f"gate{j}", [P, 3, E], F32) for j in range(TI)]
        w = [sb(f"w{j}", [P, 8], F32) for j in range(TI)]
        hg = [sb(f"hg{j}", [P, ER], F32) for j in range(TI)]
        hgt = [sb(f"hgt{j}", [P, P], F32) for j in range(TI)]
        ps = [ctx.enter_context(nc.psum_tensor(f"mix_ps{j}", [P, D], F32)) for j in range(TI)]
        base = [ctx.enter_context(nc.psum_tensor(f"mix_base{j}", [P, D], F32)) for j in range(TI)]

        consts, chain, passed = sem("consts"), sem("chain"), sem("passed")
        xin = [sem(f"xin{j}") for j in range(TI)]
        matrices, first, one, turned, one_t, lin_done = (sem(s) for s in (
            "matrices", "first", "x1", "x1_turned", "x1t", "lin"))
        margin, shares, gated, h_turned, hg_t, experts, two, last_mix, three = (sem(s) for s in (
            "margin", "shares", "gated", "h_turned", "hgt", "experts", "x2", "last_mix", "x3"))
        stored = [sem(f"stored{j}") for j in range(TI)]

        block = ctx.enter_context(nc.Block())

        @block.sync
        def _(sp):
            sp.dma_start(lin[:, :, :], lin_t.rearrange("(k p) o -> p k o", p=P)).then_inc(consts, 16)
            sp.dma_start(route[:, :, 0:E], router_t.rearrange("(k p) e -> p k e", p=P)).then_inc(consts, 16)
            sp.dma_start(route[:, :, E:ROUTE], a_t.rearrange("(k p) e -> p k e", p=P)).then_inc(consts, 16)
            sp.dma_start(low[:, :], b_t).then_inc(consts, 16)
            for j in range(TI):
                sp.dma_start(xa[j][:, :], x_v[j]).then_inc(xin[j], 16)
            with sp.Fori(0, NT - 2 * TI + 1, TI) as t:
                for j in range(TI):
                    sp.wait_ge(one, t + j + 1)
                    sp.dma_start(xa[j][:, :], x_v[ds(t + TI + j, 1)].rearrange("o p d -> (o p) d")
                                 ).then_inc(xin[j], 16)
                for j in range(TI):
                    sp.wait_ge(three, t + j + 1)
                    sp.dma_start(x3_d[ds(t + j, 1)].rearrange("o p d -> (o p) d"), xd[j][:, :]
                                 ).then_inc(stored[j], 16)
            for j in range(TI):
                sp.wait_ge(three, NT - TI + j + 1)
                sp.dma_start(x3_d[NT - TI + j], xd[j][:, :]).then_inc(stored[j], 16)
            for j in range(TI):
                sp.wait_ge(stored[j], 16 * (NT // TI + 1))

        @block.scalar
        def _(act):
            with act.Fori(0, NT - TI + 1, TI) as t:
                for j in range(TI):
                    act.wait_ge(turned, t + j + 1)
                    nc.scalar.activation(x1t[j][:, :], ps[j][:, :], ACT.Copy).then_inc(one_t, 1)
                for j in range(TI):
                    act.wait_ge(margin, t + j + 1)
                    nc.scalar.activation(w[j][:, 1:2], w[j][:, 0:1], ACT.Exp).then_inc(shares, 1)
                for j in range(TI):
                    act.wait_ge(h_turned, t + j + 1)
                    nc.scalar.activation(hgt[j][:, :], ps[j][:, 0:P], ACT.Copy).then_inc(hg_t, 1)

        @block.tensor
        def _(pe):
            mm = nc.tensor.matmul
            pe.wait_ge(consts, 4 * 16)
            with pe.Fori(0, NT - TI + 1, TI) as t:
                for j in range(TI):
                    pe.wait_ge(xin[j], 4 * t + 16)
                    pe.wait_ge(matrices, t + j + 1)
                    mm(ps[j][:, :], m0[j][:, :, :].rearrange("p b d -> p (b d)"), xa[j][:, :], start=True,
                       stop=True).then_inc(first, 1)
                for j in range(TI):
                    pe.wait_ge(one, t + j + 1)
                    for k in range(KD):
                        last = nc.tensor.transpose(ps[j][:, k * P:(k + 1) * P], xb[j][:, k * P:(k + 1) * P],
                                                   ident[:, :])
                    last.then_inc(turned, 1)
                for j in range(TI):
                    pe.wait_ge(one_t, t + j + 1)
                    for k in range(KD):
                        mm(ps[j][:, 0:ROUTE], x1t[j][:, k * P:(k + 1) * P], route[:, k, :], start=(k == 0),
                           stop=(k == KD - 1))
                        last = mm(base[j][:, :], x1t[j][:, k * P:(k + 1) * P], lin[:, k, :], start=(k == 0),
                                  stop=False)
                    last.then_inc(lin_done, 1)
                for j in range(TI):
                    pe.wait_ge(gated, t + j + 1)
                    nc.tensor.transpose(ps[j][:, 0:P], hg[j][:, :], ident[:, :]).then_inc(h_turned, 1)
                for j in range(TI):
                    pe.wait_ge(hg_t, t + j + 1)
                    mm(base[j][:, :], hgt[j][:, :], low[:, :], start=False, stop=True).then_inc(experts, 1)
                for j in range(TI):
                    pe.wait_ge(two, t + j + 1)
                    mm(ps[j][:, :], m2[j][:, :, :].rearrange("p b d -> p (b d)"), xc[j][:, :], start=True,
                       stop=True).then_inc(last_mix, 1)

        STEPS = 14

        @block.vector
        def _(dve):
            v = nc.vector
            for j in range(TI):
                dve.sem_inc(stored[j], 16)
            with dve.Fori(0, NT - TI + 1, TI) as t:
                n = [0]

                def step(op, alone=False):
                    for j in range(TI):
                        if alone:
                            hold(dve, chain, t * STEPS + (n[0] - 1) * TI + j + 1, passed)
                        else:
                            dve.wait_ge(chain, t * STEPS + (n[0] - 1) * TI + j + 1)
                        op(j).then_inc(chain, 1)
                    n[0] += 1

                for j in range(TI):
                    for m, g in ((m0, g0), (m2, g2)):
                        last = v.tensor_tensor(m[j][:, :, :], g[:, ds(t + j, 1), :].to_broadcast([P, BT, MIX]),
                                               blocks[:, :, :], ALU.mult)
                    last.then_inc(matrices, 1)
                for j in range(TI):
                    dve.wait_ge(first, t + j + 1)
                    v.tensor_tensor(xb[j][:, :], ps[j][:, :], xa[j][:, :], ALU.add).then_inc(one, 1)
                for j in range(TI):
                    dve.wait_ge(lin_done, t + j + 1)
                    v.tensor_tensor(logit[j][:, :], ps[j][:, 0:E], bias[:, ds(t + j, 1), :].rearrange(
                        "p o e -> p (o e)"), ALU.add).then_inc(chain, 1)
                n[0] = 1
                step(lambda j: v.max(top[j][:, :], logit[j][:, :]), alone=True)
                step(lambda j: v.max_index(top_i[j][:, :], top[j][:, :], logit[j][:, :]), alone=True)
                step(lambda j: v.tensor_copy(top_f[j][:, 0:2], top_i[j][:, 0:2]))
                step(lambda j: v.tensor_scalar(out=gate[j][:, 0, :], in0=iota8[:, :], scalar1=top_f[j][:, 0:1],
                                               scalar2=None, op0=ALU.is_equal))
                step(lambda j: v.tensor_scalar(out=gate[j][:, 1, :], in0=iota8[:, :], scalar1=top_f[j][:, 1:2],
                                               scalar2=None, op0=ALU.is_equal))
                step(lambda j: v.tensor_tensor(w[j][:, 0:1], top[j][:, 1:2], top[j][:, 0:1], ALU.subtract))
                for j in range(TI):
                    dve.wait_ge(chain, t * STEPS + (n[0] - 1) * TI + j + 1)
                    v.tensor_copy(w[j][:, 6:7], w[j][:, 0:1]).then_inc(margin, 1)
                for j in range(TI):
                    dve.wait_ge(shares, t + j + 1)
                    v.tensor_scalar(out=w[j][:, 2:3], in0=w[j][:, 1:2], scalar1=1.0, scalar2=None,
                                    op0=ALU.add).then_inc(chain, 1)
                n[0] += 1
                step(lambda j: v.reciprocal(w[j][:, 3:4], w[j][:, 2:3]))
                step(lambda j: v.tensor_scalar(out=w[j][:, 4:5], in0=w[j][:, 3:4], scalar1=LORA, scalar2=None,
                                               op0=ALU.mult))
                step(lambda j: v.tensor_tensor(w[j][:, 5:6], w[j][:, 4:5], w[j][:, 1:2], ALU.mult))
                step(lambda j: v.tensor_scalar(out=gate[j][:, 1, :], in0=gate[j][:, 1, :], scalar1=w[j][:, 5:6],
                                               scalar2=None, op0=ALU.mult))
                step(lambda j: v.scalar_tensor_tensor(out=gate[j][:, 2, :], in0=gate[j][:, 0, :],
                                                      scalar=w[j][:, 4:5], in1=gate[j][:, 1, :], op0=ALU.mult,
                                                      op1=ALU.add))
                step(lambda j: v.tensor_tensor(hg[j][:, :].rearrange("p (e r) -> p e r", r=R),
                                               ps[j][:, E:ROUTE].rearrange("p (e r) -> p e r", r=R),
                                               gate[j][:, 2, :].unsqueeze(2).to_broadcast([P, E, R]), ALU.mult))
                assert n[0] == STEPS
                for j in range(TI):
                    dve.wait_ge(chain, t * STEPS + (STEPS - 1) * TI + j + 1)
                    dve.sem_inc(gated, 1)
                for j in range(TI):
                    dve.wait_ge(experts, t + j + 1)
                    v.tensor_tensor(xc[j][:, :], base[j][:, :], xb[j][:, :], ALU.add).then_inc(two, 1)
                for j in range(TI):
                    dve.wait_ge(last_mix, t + j + 1)
                    dve.wait_ge(stored[j], 4 * t + 16)
                    v.tensor_tensor(xd[j][:, :], ps[j][:, :], xc[j][:, :], ALU.add).then_inc(three, 1)


def splitting(nc, up, wh, wl, wq_t, wk_t, wv_t, wo_t, k_t, v_rows, k_d, v_d, wo_d):
    ctx = ExitStack()
    with ctx:
        def sem(name):
            return ctx.enter_context(nc.semaphore("split_" + name))

        NB = 4
        raw = [ctx.enter_context(nc.sbuf_tensor(f"split_raw{i}", [P, SC], F32)) for i in range(NB)]
        two = [ctx.enter_context(nc.sbuf_tensor(f"split_two{i}", [P, 2 * SC], F16)) for i in range(NB)]
        loaded = [sem(f"loaded{i}") for i in range(NB)]
        stored = [sem(f"stored{i}") for i in range(NB)]
        high, low = sem("high"), sem("low")
        CK = SC // (HK * PS)
        CO = SC // D
        NC = PAGES // CK

        def one(tile, c):
            return tile[ds(c, 1)]

        k_c = k_t.rearrange("(c n) p m -> c p n m", n=CK)
        v_c = v_rows.rearrange("(c p) m -> c p m", p=P)
        wo_c = wo_t.rearrange("(c n p) m -> c p n m", p=P, n=CO)
        kd_c = k_d.rearrange("(c n) p m -> c p n m", n=CK)
        vd_c = v_d.rearrange("(c p) m -> c p m", p=P)
        wod_c = wo_d.rearrange("p (c n) h m -> c p n (h m)", n=CO)
        weights = [(w, at, k, c) for w, at, n in ((wq_t, 0, NQ), (wk_t, NQ, NKV), (wv_t, NQ + NKV, NKV))
                   for k in range(KD) for c in range(0, n, SC)]
        NWC = len(weights)
        assert NWC % NB == 0
        def load(sp, kind, c):
            src = one((k_c, v_c, wo_c)[kind], c)
            if kind == 1:
                sp.dma_start(raw[1][:, :], src.rearrange("o p m -> (o p) m")).then_inc(loaded[1], 16)
            else:
                n = (CK, None, CO)[kind]
                sp.dma_start(raw[kind][:, :].rearrange("p (n m) -> p n m", n=n),
                             src.rearrange("o p n m -> (o p) n m")).then_inc(loaded[kind], 16)

        def store(sp, kind, c):
            dst = one((kd_c, vd_c, wod_c)[kind], c)
            if kind == 1:
                sp.dma_start(dst.rearrange("o p m -> (o p) m"), two[1][:, :]).then_inc(stored[1], 16)
            else:
                n = (CK, None, CO)[kind]
                sp.dma_start(dst.rearrange("o p n m -> (o p) n m"),
                             two[kind][:, :].rearrange("p (n m) -> p n m", n=n)).then_inc(stored[kind], 16)

        block = ctx.enter_context(nc.Block())

        def views(kind, i):
            if kind == 0:
                a = raw[i][:, :].rearrange("p (n m) -> p n m", m=PS)
                b = two[i][:, :].rearrange("p (n h m) -> p n h m", h=2, m=PS)
            elif kind == 1:
                a = raw[i][:, :].rearrange("p (n m) -> p n m", m=HD)
                b = two[i][:, :].rearrange("p (n h m) -> p n h m", h=2, m=HD)
            else:
                a = raw[i][:, :].rearrange("p (n m) -> p n m", m=D)
                b = two[i][:, :].rearrange("p (n h m) -> p n h m", h=2, m=D)
            return a, b[:, :, 0, :], b[:, :, 1, :]

        @block.sync
        def _(sp):
            for i, (w, at, k, c) in enumerate(weights):
                if i >= NB:
                    sp.wait_ge(high, i - NB + 1)
                    sp.wait_ge(low, i - NB + 1)
                sp.dma_start(raw[i % NB][:, :], w[k * P:(k + 1) * P, c:c + SC]).then_inc(loaded[i % NB], 16)
            first = NWC // NB * 16
            for kind in range(3):
                sp.wait_ge(high, NWC - NB + kind + 1)
                sp.wait_ge(low, NWC - NB + kind + 1)
                load(sp, kind, 0)
            with sp.Fori(0, NC - 1) as c:
                for kind in range(3):
                    sp.wait_ge(high, 3 * c + (NWC + kind + 1))
                    sp.wait_ge(low, 3 * c + (NWC + kind + 1))
                    store(sp, kind, c)
                    load(sp, kind, c + 1)
            for kind in range(3):
                sp.wait_ge(high, 3 * (NC - 1) + NWC + kind + 1)
                sp.wait_ge(low, 3 * (NC - 1) + NWC + kind + 1)
                store(sp, kind, NC - 1)
            for kind in range(3):
                sp.wait_ge(stored[kind], 16 * (NC + 1))

        @block.scalar
        def _(act):
            for i, (w, at, k, c) in enumerate(weights):
                act.wait_ge(loaded[i % NB], 16 * (i // NB + 1))
                nc.scalar.activation(wh[:, k, at + c:at + c + SC], raw[i % NB][:, :], ACT.Copy,
                                     scale=up[:, 3:4]).then_inc(high, 1)
            for kind in range(3):
                act.sem_inc(stored[kind], 16)
            with act.Fori(0, NC) as c:
                for kind in range(3):
                    act.wait_ge(loaded[kind], 16 * c + 16 * (NWC // NB + 1))
                    act.wait_ge(stored[kind], 16 * c + 16)
                    a, h, _ = views(kind, kind)
                    nc.scalar.activation(h, a, ACT.Copy, scale=up[:, kind:kind + 1]).then_inc(high, 1)

        @block.vector
        def _(dve):
            for i, (w, at, k, c) in enumerate(weights):
                dve.wait_ge(high, i + 1)
                nc.vector.scalar_tensor_tensor(out=wl[:, k, at + c:at + c + SC], in0=raw[i % NB][:, :],
                                               scalar=up[:, 3:4], in1=wh[:, k, at + c:at + c + SC], op0=ALU.mult,
                                               op1=ALU.subtract).then_inc(low, 1)
            with dve.Fori(0, NC) as c:
                for kind in range(3):
                    dve.wait_ge(high, 3 * c + (NWC + kind + 1))
                    a, h, lo = views(kind, kind)
                    nc.vector.scalar_tensor_tensor(out=lo, in0=a, scalar=up[:, kind:kind + 1], in1=h,
                                                   op0=ALU.mult, op1=ALU.subtract).then_inc(low, 1)


def projections(nc, ident, ident16, up, down, vw, cos, sin, wa, wb, wh, wl, x3_d, q_d, kn_d, vn_d):
    ctx = ExitStack()
    with ctx:
        def sb(name, shape, dt):
            return ctx.enter_context(nc.sbuf_tensor("proj_" + name, shape, dt))

        def sem(name):
            return ctx.enter_context(nc.semaphore("proj_" + name))

        x3 = [sb(f"x3{i}", [P, D], F32) for i in range(2)]
        col = [sb(f"col{i}", [P, 12], F32) for i in range(2)]
        xh = sb("xh", [P, D], F16)
        xl = sb("xl", [P, D], F16)
        xt = [sb(f"xt{i}", [P, KD, 2, P], F16) for i in range(2)]
        raw = [sb(f"raw{i}", [P, ROT, D], F32) for i in range(2)]
        sq = [sb(f"sq{i}", [P, D], F32) for i in range(2)]
        ss = sb("ss", [P, 4, HALVES], F32)
        inv = [sb(f"inv{i}", [P, HALVES], F32) for i in range(2)]
        ta = sb("ta", [P, 2, HD], F32)
        tb = sb("tb", [P, 2, HD], F32)
        ra = [sb(f"ra{i}", [P, D], F32) for i in range(2)]
        rb = [sb(f"rb{i}", [P, D], F32) for i in range(2)]
        rn = [sb(f"rn{i}", [P, D], F32) for i in range(2)]
        turned = [sb(f"turned{i}", [P, 2 * D], F16) for i in range(2)]
        v32 = [sb(f"v32{i}", [P, D], F32) for i in range(VB)]
        vp = sb("vp", [P, 3, NKV], BF16)
        blk = [ctx.enter_context(nc.psum_tensor(f"proj_blk{i}", [P, D], F32)) for i in range(3)]
        tq = [ctx.enter_context(nc.psum_tensor(f"proj_tq{i}", [P, D], F32)) for i in range(2)]
        xp = ctx.enter_context(nc.psum_tensor("proj_xp", [P, 2 * D], F16))

        xin = [sem(f"xin{i}") for i in range(2)]
        xchain, scaled, xhigh, xlow, xturned, xt_done = (sem(s) for s in (
            "xchain", "x_scaled", "x_high", "x_low", "x_turned", "xt"))
        blk_done, blk_free, ss_done, chain, rooted, inv_done = (sem(s) for s in (
            "block", "block_read", "squares", "chain", "rooted", "inverse"))
        root_in = sem("mean")
        tab_done, ra_done, rb_done, sum_done, rn_done, tq_done, high, low = (sem(s) for s in (
            "tables", "first_product", "second_product", "rotated", "normalised", "heads_turned",
            "heads_high", "heads_low"))
        out_q = [sem(f"stored{i}") for i in range(2)]
        rest1, vmid, vlow, v_out = sem("v_rest"), sem("v_mid"), sem("v_low"), sem("v_stored")
        XSTEPS, CSTEPS = 7, 4

        def head_views(n):
            if n < QB:
                src = tq[n % 2][:, :].rearrange("p (h b s) -> p b h s", h=HB, b=BT)
                dst = turned[n % 2][:, :].rearrange("p (b two h s) -> p b two h s", b=BT, two=2, h=HB)
                return src, dst[:, :, 0], dst[:, :, 1]
            src = tq[n % 2][:, :].rearrange("p (h b s) -> p b h s", h=HB, b=BT)
            dst = turned[n % 2][:, :].rearrange("p (b h two s) -> p b h two s", b=BT, two=2, h=HB)
            return src, dst[:, :, :, 0], dst[:, :, :, 1]

        block = ctx.enter_context(nc.Block())

        def tiles(engine, body):
            body(0, 0)
            body(1, 1)
            with engine.Fori(2, NT - 3, 2) as t:
                body(t, 0)
                body(t + 1, 1)
            body(NT - 2, 0)
            body(NT - 1, 1)

        def is_tile(t, n):
            return isinstance(t, int) and t == n

        @block.sync
        def _(sp):
            for i in range(2):
                sp.dma_start(x3[i][:, :], x3_d[i]).then_inc(xin[i], 16)

            def store_heads(t, n):
                idx = t * ROT + n
                sp.wait_ge(high, idx + 1)
                sp.wait_ge(low, idx + 1)
                src = turned[n % 2][:, :]
                if n < QB:
                    dst = q_d[ds(t, 1), n].rearrange("o p b c -> (o p) b c")
                    src = src.rearrange("p (b c) -> p b c", b=BT)
                else:
                    w = PG // KB
                    dst = kn_d[ds(t * BT, BT), :, (n - QB) * w:(n - QB + 1) * w].rearrange("b p c -> p b c")
                    src = src.rearrange("p (b c) -> p b c", b=BT)
                sp.dma_start(dst, src).then_inc(out_q[n % 2], 16)

            def store_values(t):
                sp.wait_ge(vmid, (t + 1) * VB)
                sp.wait_ge(vlow, (t + 1) * VB)
                for r, part in enumerate((0, 1, 2, 0)):
                    for b in range(BT):
                        sp.dma_start(vn_d[ds(t * BT + b, 1), r * S:(r + 1) * S, :].rearrange("o s c -> (o s) c"),
                                     vp[b * S:(b + 1) * S, part, :]).then_inc(v_out, 16)

            def body(t, p):
                for n in range(BLK):
                    if not is_tile(t, 0) and n < ROT:
                        store_heads(t - 1, n)
                        if n == 3:
                            store_values(t - 1)
                    if n == 4 and not is_tile(t, NT - 2) and not is_tile(t, NT - 1):
                        sp.wait_ge(xhigh, t + 1)
                        sp.wait_ge(xlow, t + 1)
                        sp.dma_start(x3[p][:, :], x3_d[ds(t + 2, 1)].rearrange("o p d -> (o p) d")
                                     ).then_inc(xin[p], 16)

            tiles(sp, body)
            for n in range(ROT):
                store_heads(NT - 1, n)
                if n == 3:
                    store_values(NT - 1)
            for i in range(2):
                sp.wait_ge(out_q[i], 16 * (NT * ROT // 2))
            sp.wait_ge(v_out, 16 * NT * BT * 4)

        @block.tensor
        def _(pe):
            mm = nc.tensor.matmul

            def turn_x(t, p):
                pe.wait_ge(xhigh, t + 1)
                pe.wait_ge(xlow, t + 1)
                after(pe, xt_done, t)
                for k in range(KD):
                    for h, part in enumerate((xh, xl)):
                        at = (2 * k + h) * P
                        last = nc.tensor.transpose(xp[:, at:at + P], part[:, k * P:(k + 1) * P], ident16[:, :])
                last.then_inc(xturned, 1)

            def turn_heads(t, n):
                idx = t * ROT + n
                pe.wait_ge(rn_done, idx + 1)
                after(pe, high, idx - 1)
                after(pe, low, idx - 1)
                for h in range(HB):
                    last = nc.tensor.transpose(tq[n % 2][:, h * P:(h + 1) * P], rn[n % 2][:, h * P:(h + 1) * P],
                                               ident[:, :])
                last.then_inc(tq_done, 1)

            def body(t, p):
                pe.wait_ge(xt_done, t + 1)
                for n in range(BLK):
                    after(pe, blk_free, t * BLK + n - 2)
                    out = blk[n % 3][:, :]
                    cols = slice(n * D, (n + 1) * D)
                    for k in range(KD):
                        mm(out, xt[p][:, k, 0, :], wh[:, k, cols], start=(k == 0), stop=False)
                        mm(out, xt[p][:, k, 0, :], wl[:, k, cols], start=False, stop=False)
                        last = mm(out, xt[p][:, k, 1, :], wh[:, k, cols], start=False, stop=(k == KD - 1))
                    last.then_inc(blk_done, 1)
                    if not is_tile(t, 0) and 1 <= n <= ROT:
                        turn_heads(t - 1, n - 1)
                    if n == ROT and not is_tile(t, NT - 1):
                        turn_x(t + 1, 1 - p)

            turn_x(0, 0)
            tiles(pe, body)
            for n in range(ROT):
                turn_heads(NT - 1, n)

        @block.scalar
        def _(act):
            copy = lambda out, in_, **kw: nc.scalar.activation(out, in_, ACT.Copy, **kw)

            def x_high(t, p):
                act.wait_ge(scaled, t + 1)
                after(act, xturned, t)
                copy(xh[:, :], x3[p][:, :], scale=col[p][:, 2:3]).then_inc(xhigh, 1)

            def heads_high(t, n):
                idx = t * ROT + n
                act.wait_ge(tq_done, idx + 1)
                after(act, out_q[n % 2], (t * (ROT // 2) + n // 2) * 16)
                src, dst, _ = head_views(n)
                copy(dst, src).then_inc(high, 1)

            def normalise(t, p, n):
                idx = t * ROT + n
                act.wait_ge(sum_done, idx + 1)
                if n == 0:
                    act.wait_ge(inv_done, t + 1)
                after(act, tq_done, idx - 1)
                for h in range(HB):
                    cols = slice(h * HD, (h + 1) * HD)
                    last = copy(rn[n % 2][:, cols], rb[n % 2][:, cols],
                                scale=inv[p][:, n * HB + h:n * HB + h + 1])
                last.then_inc(rn_done, 1)

            def middle(t, j):
                act.wait_ge(rest1, t * VB + j + 1)
                copy(vp[:, 1, j * D:(j + 1) * D], v32[j][:, :]).then_inc(vmid, 1)

            def behind(t, p, n):
                if n >= 2:
                    heads_high(t, n - 2)
                if n < ROT:
                    normalise(t, p, n)
                if 1 <= n <= VB:
                    middle(t, n - 1)

            def body(t, p):
                for n in range(BLK):
                    if n == BLK - 1:
                        act.wait_ge(root_in, t + 1)
                        nc.scalar.activation(ss[:, 2, :], ss[:, 1, :], ACT.Sqrt).then_inc(rooted, 1)
                    if not is_tile(t, 0):
                        behind(t - 1, 1 - p, n)
                    act.wait_ge(blk_done, t * BLK + n + 1)
                    if n < ROT:
                        after(act, sum_done, (t - 2) * ROT + n + 1)
                        copy(raw[p][:, n, :], blk[n % 3][:, :])
                        after(act, ss_done, t * ROT + n - 1)
                        nc.scalar.activation(sq[n % 2][:, :], blk[n % 3][:, :], ACT.Square).then_inc(blk_free, 1)
                    else:
                        j = n - ROT
                        after(act, v_out, t * BT * 4 * 16)
                        after(act, vlow, t * VB)
                        copy(v32[j][:, :], blk[n % 3][:, :], scale=col[p][:, 6:7])
                        copy(vp[:, 0, j * D:(j + 1) * D], blk[n % 3][:, :], scale=col[p][:, 6:7]
                             ).then_inc(blk_free, 1)
                    if n == ROT - 2 and not is_tile(t, NT - 1):
                        x_high(t + 1, 1 - p)

            x_high(0, 0)
            tiles(act, body)
            for n in range(ROT + 2):
                behind(NT - 1, 1, n)

        @block.gpsimd
        def _(pool):
            g = nc.gpsimd

            def tables(t):
                after(pool, sum_done, t * ROT)
                for i in range(2):
                    for tab, trig, w in ((ta, cos, wa), (tb, sin, wb)):
                        last = g.tensor_tensor(tab[:, i, :].rearrange("p (h c) -> p h c", h=2),
                                               trig[:, ds(t, 1), :].to_broadcast([P, 2, HALF]),
                                               w[:, i, :].rearrange("p (h c) -> p h c", h=2), ALU.mult)
                last.then_inc(tab_done, 1)
                pool.wait_ge(tab_done, t + 1)

            def first_product(t, p, n):
                idx = t * ROT + n
                after(pool, sum_done, idx - 1)
                pool.wait_ge(blk_free, t * BLK + n + 1)
                g.tensor_tensor(ra[n % 2][:, :].rearrange("p (h c) -> p h c", h=HB),
                                raw[p][:, n, :].rearrange("p (h c) -> p h c", h=HB),
                                ta[:, n // QB, :].unsqueeze(1).to_broadcast([P, HB, HD]), ALU.mult
                                ).then_inc(ra_done, 1)

            def rest(t, j):
                pool.wait_ge(blk_free, t * BLK + ROT + j + 1)
                g.tensor_tensor(v32[j][:, :], v32[j][:, :], vp[:, 0, j * D:(j + 1) * D], ALU.subtract
                                ).then_inc(rest1, 1)

            def rest_low(t, j):
                pool.wait_ge(vmid, t * VB + j + 1)
                g.tensor_tensor(vp[:, 2, j * D:(j + 1) * D], v32[j][:, :], vp[:, 1, j * D:(j + 1) * D],
                                ALU.subtract).then_inc(vlow, 1)

            def behind(t, p):
                for n in range(ROT):
                    first_product(t, p, n)
                    if n < VB:
                        rest(t, n)
                    elif n < 2 * VB:
                        rest_low(t, n - VB)

            def body(t, p):
                if not is_tile(t, 0):
                    behind(t - 1, 1 - p)
                tables(t)

            tiles(pool, body)
            behind(NT - 1, 1)

        @block.vector
        def _(dve):
            v = nc.vector

            def scales(t, p):
                c = col[p]
                n = [0]

                def step(ins):
                    n[0] += 1
                    ins.then_inc(xchain, 1)
                    dve.wait_ge(xchain, t * XSTEPS + n[0])

                dve.wait_ge(xin[p], 8 * t + 8 * (2 - p))
                step(v.tensor_reduce(c[:, 0:1], x3[p][:, :], AX.X, ALU.max, apply_absolute_value=True))
                step(v.tensor_scalar(out=c[:, 0:1], in0=c[:, 0:1], scalar1=TINY, scalar2=None, op0=ALU.max))
                step(v.tensor_scalar(out=c[:, 1:2].bitcast(I32), in0=c[:, 0:1].bitcast(I32), scalar1=EXPONENT,
                                     scalar2=None, op0=ALU.bitwise_and))
                step(v.reciprocal(c[:, 3:4], c[:, 1:2]))
                step(v.tensor_scalar(out=c[:, 2:3], in0=c[:, 3:4], scalar1=TOP, scalar2=None, op0=ALU.mult))
                step(v.tensor_scalar(out=c[:, 6:7], in0=c[:, 1:2], scalar1=1.0 / TOP, scalar2=vw[:, :],
                                     op0=ALU.mult, op1=ALU.mult))
                step(v.tensor_tensor(c[:, 4:5], c[:, 2:3], up[:, 3:4], ALU.mult))
                v.scalar_tensor_tensor(out=c[:, 5:6], in0=c[:, 4:5], scalar=EPS, in1=c[:, 4:5], op0=ALU.mult,
                                       op1=ALU.mult).then_inc(scaled, 1)
                assert n[0] == XSTEPS

            def x_low(t, p):
                dve.wait_ge(xhigh, t + 1)
                after(dve, xturned, t)
                v.scalar_tensor_tensor(out=xl[:, :], in0=x3[p][:, :], scalar=col[p][:, 2:3], in1=xh[:, :],
                                       op0=ALU.mult, op1=ALU.subtract).then_inc(xlow, 1)

            def keep_xt(t, p):
                dve.wait_ge(xturned, t + 1)
                v.tensor_copy(xt[p][:, :, :, :].rearrange("p k h c -> p (k h c)"), xp[:, :]).then_inc(xt_done, 1)

            def squares(t, n):
                dve.wait_ge(blk_free, t * BLK + n + 1)
                v.tensor_reduce(ss[:, 0, n * HB:(n + 1) * HB], sq[n % 2][:, :].rearrange("p (h c) -> p h c", h=HB),
                                AX.X, ALU.add).then_inc(ss_done, 1)

            def mean(t, p):
                dve.wait_ge(ss_done, (t + 1) * ROT)
                v.tensor_scalar(out=ss[:, 1, :], in0=ss[:, 0, :], scalar1=1.0 / HD, scalar2=col[p][:, 5:6],
                                op0=ALU.mult, op1=ALU.add).then_inc(root_in, 1)

            def inverse(t, p):
                n = [0]

                def step(ins):
                    n[0] += 1
                    ins.then_inc(chain, 1)
                    dve.wait_ge(chain, t * CSTEPS + n[0])

                after(dve, rn_done, (t - 1) * ROT)
                dve.wait_ge(rooted, t + 1)
                step(v.reciprocal(ss[:, 3, :], ss[:, 2, :]))
                step(v.tensor_tensor(ss[:, 2, :], ss[:, 3, :], ss[:, 1, :], ALU.mult))
                step(v.tensor_tensor(ss[:, 2, :], ss[:, 2, :], ss[:, 3, :], ALU.mult))
                step(v.tensor_scalar(out=ss[:, 2, :], in0=ss[:, 2, :], scalar1=-0.5, scalar2=1.5, op0=ALU.mult,
                                     op1=ALU.add))
                v.tensor_tensor(inv[p][:, :], ss[:, 2, :], ss[:, 3, :], ALU.mult).then_inc(inv_done, 1)
                dve.wait_ge(inv_done, t + 1)
                assert n[0] == CSTEPS

            def rotate(t, p, n):
                idx = t * ROT + n
                src = raw[p][:, n, :].rearrange("p (h two c) -> p h two c", h=HB, two=2)
                dst = rb[n % 2][:, :].rearrange("p (h two c) -> p h two c", h=HB, two=2)
                after(dve, rn_done, idx - 1)
                for half in range(2):
                    table = tb[:, n // QB, half * HALF:(half + 1) * HALF].unsqueeze(1).to_broadcast([P, HB, HALF])
                    last = v.tensor_tensor(dst[:, :, half, :], src[:, :, 1 - half, :], table, ALU.mult)
                last.then_inc(rb_done, 1)

            def add(t, n):
                idx = t * ROT + n
                dve.wait_ge(rb_done, idx + 1)
                dve.wait_ge(ra_done, idx + 1)
                v.tensor_tensor(rb[n % 2][:, :], rb[n % 2][:, :], ra[n % 2][:, :], ALU.add).then_inc(sum_done, 1)

            def heads_low(t, n):
                dve.wait_ge(high, t * ROT + n + 1)
                src, hi, lo = head_views(n)
                v.tensor_tensor(lo, src, hi, ALU.subtract).then_inc(low, 1)

            def body(t, p):
                if not is_tile(t, 0):
                    dve.wait_ge(tab_done, t)
                for n in range(BLK):
                    if not is_tile(t, 0):
                        if n < ROT:
                            rotate(t - 1, 1 - p, n)
                            add(t - 1, n)
                        if n >= 2:
                            heads_low(t - 1, n - 2)
                    if 1 <= n <= ROT:
                        squares(t, n - 1)
                    if not is_tile(t, NT - 1):
                        if n == 5:
                            scales(t + 1, 1 - p)
                        if n == ROT - 1:
                            x_low(t + 1, 1 - p)
                        if n == ROT:
                            keep_xt(t + 1, 1 - p)
                    if n == ROT:
                        mean(t, p)
                    if n == BLK - 1:
                        inverse(t, p)

            scales(0, 0)
            x_low(0, 0)
            keep_xt(0, 0)
            tiles(dve, body)
            dve.wait_ge(tab_done, NT)
            for n in range(ROT + 2):
                if n < ROT:
                    rotate(NT - 1, 1, n)
                    add(NT - 1, n)
                if n >= 2:
                    heads_low(NT - 1, n - 2)


def attention(nc, ident, cs, oscale, v_idx, lens_f, page_row, k_d, v_d, kn_d, vn_d, q_d, wo_d, x3_d, out_v):
    U = BT * HK
    QUAD = 4
    START = 1
    ctx = ExitStack()
    with ctx:
        def sb(name, shape, dt):
            return ctx.enter_context(nc.sbuf_tensor("att_" + name, shape, dt))

        def sem(name):
            return ctx.enter_context(nc.semaphore("att_" + name))

        wo = sb("wo", [P, HQ, 2, D], F16)
        keys = [sb(f"keys{i}", [P, NPP + 1, HK, 2, PS], F16) for i in range(2)]
        values = [sb(f"values{i}", [P, LC, HK, 2, HD], F16) for i in range(2)]
        fresh = [sb(f"fresh{i}", [P, HK, HD], BF16) for i in range(2)]
        query = [sb(f"query{i}", [P, HK, 2, P], F16) for i in range(2)]
        idx = [sb(f"idx{i}", [P, LC], U32) for i in range(2)]
        iota = sb("iota", [P, L], F16)
        mask = [sb(f"mask{i}", [P, S + L + S], F32) for i in range(2)]
        prob = [sb(f"prob{i}", [P, LK], F32) for i in range(2)]
        norm = [sb(f"norm{i}", [P, L + P], F32) for i in range(2)]
        col = [sb(f"col{i}", [P, 4], F32) for i in range(2)]
        tph = [sb(f"tph{i}", [P, L + P], F16) for i in range(2)]
        tpl = [sb(f"tpl{i}", [P, L], F16) for i in range(2)]
        ot = [sb(f"ot{i}", [P, 2, HQ, P], BF16) for i in range(2)]
        of = sb("of", [P, D], F32)
        res = [sb(f"res{i}", [P, D], F32) for i in range(2)]
        iota_i = prob[0][:, 0:L].bitcast(I32)
        banks = ctx.enter_context(nc.psum_tensor("att_scores", [P, 3 * D], F32))
        sc = [banks[:, 0:LK], banks[:, 3 * D - LK:3 * D]]
        tr = [ctx.enter_context(nc.psum_tensor(f"att_tr{i}", [P, D], F32)) for i in range(2)]
        tr_new = ctx.enter_context(nc.psum_tensor("att_tr_new", [P, D], F32))
        o_ps = ctx.enter_context(nc.psum_tensor("att_o", [P, D], F32))
        y_ps = ctx.enter_context(nc.psum_tensor("att_y", [P, D], F32))

        wo_in, iota_int, iota_done, unmasked = sem("wo_in"), sem("iota_int"), sem("iota"), sem("unmasked")
        kq_in = [sem(f"keys_in{i}") for i in range(2)]
        vc_in = [sem(f"values_in{i}") for i in range(2)]
        vn_in = [sem(f"fresh_in{i}") for i in range(2)]
        x_in = [sem(f"x_in{i}") for i in range(2)]
        stored = [sem(f"stored{i}") for i in range(2)]
        idx_done, idx_seen, qk_seen = sem("idx"), sem("idx_seen"), sem("scores_seen")
        mask_done, qk_done, max_done, nb_done, exp_done = (sem(s) for s in (
            "mask", "scores", "max", "neg_max", "exp"))
        inv_done, norm_done, new_done = (sem(s) for s in ("sum_inverse", "normalised", "new_normalised"))
        tr_done, th_done, tl_done, pv_done = (sem(s) for s in ("turned", "high", "low", "weighted"))
        o_kept, oh_done, ol_done, y_done, res_done = (sem(s) for s in (
            "out", "out_high", "out_low", "projected", "result"))
        def quad_of_step(do, t, i, p):
            k = (i - 7) // QUAD
            if k < 0:
                do(t - 1, k + U // QUAD, 1 - p)
            else:
                do(t, k, p)

        def quad_views(k, p):
            bi, half = divmod(k, HK // QUAD)
            heads = slice(half * QUAD * REP, (half + 1) * QUAD * REP)
            src = of[:, :].rearrange("p (h s) -> p h s", s=S)
            return src, [ot[p][:, a, heads, bi * S:(bi + 1) * S] for a in range(2)]

        block = ctx.enter_context(nc.Block())

        def groups(engine, body):
            body(0, 0, 0)
            body(1, 1, 1)
            with engine.Fori(2, NT - 1, 2) as t:
                body(t, 0, 2)
                body(t + 1, 1, 2)

        def cached(q):
            return (slice(0, L), slice(L, LK)) if q == 0 else (slice(S, LK), slice(0, S))

        def heads_of_step(i):
            n = U - START
            j = i - START
            return range(j * HQ // n, (j + 1) * HQ // n) if j >= 0 else range(0)

        @block.sync
        def _(sp):
            def load(t, bi):
                p = bi % 2
                b = t * BT + bi
                after(sp, qk_done, (b - 1) * HK)
                for half in range(2):
                    _, pages = nc.values_load_multi_w_load_instructions(
                        page_row[0:1, ds(b * NPP + half * (NPP // 2), NPP // 2)], engines=(SP,), min_val=0,
                        max_val=PAGES - 1, skip_runtime_bounds_check_because="page numbers are below PAGES")
                    for j, page in enumerate(pages):
                        sp.dma_start(keys[p][:, half * (NPP // 2) + j].rearrange("p h two s -> p (h two s)"),
                                     k_d[ds(page, 1)].rearrange("o p m -> (o p) m")).then_inc(kq_in[p], 16)
                sp.dma_start(keys[p][:, NPP].rearrange("p h two s -> p (h two s)"),
                             kn_d[ds(b, 1)].rearrange("o p m -> (o p) m")).then_inc(kq_in[p], 16)
                sp.dma_start(query[p][:, :, :, :].rearrange("p h two c -> p h (two c)"),
                             q_d[ds(t, 1), :, :, bi, :].rearrange("o g p c -> p (o g) c")).then_inc(kq_in[p], 16)
                after(sp, pv_done, (b - 1) * HK)
                sp.dma_start(fresh[p][:, :, :].rearrange("p h c -> p (h c)"),
                             vn_d[ds(b, 1)].rearrange("o p c -> (o p) c")).then_inc(vn_in[p], 16)

            def result(t, p):
                sp.wait_ge(res_done, t + 1)
                sp.dma_start(out_v[ds(t, 1)].rearrange("o p d -> (o p) d"), res[p][:, :]).then_inc(stored[p], 16)

            def body(t, p, past):
                for bi in range(BT):
                    load(t, bi)
                    if bi == 0 and past == 0:
                        sp.dma_start(wo[:, :, :, :], wo_d).then_inc(wo_in, 16)
                    if bi == 1 and past == 2:
                        result(t - 2, p)
                after(sp, stored[p], 8 * t - 8 * p)
                sp.dma_start(res[p][:, :], x3_d[ds(t, 1)].rearrange("o p d -> (o p) d")).then_inc(x_in[p], 16)

            groups(sp, body)
            result(NT - 2, 0)
            result(NT - 1, 1)
            for p in range(2):
                sp.wait_ge(stored[p], 16 * (NT // 2))

        @block.gpsimd
        def _(pool):
            g = nc.gpsimd
            g.iota(iota_i, pattern=[[1, L]], base=0, channel_multiplier=0).then_inc(iota_int, 1)
            pool.wait_ge(iota_int, 1)
            g.tensor_copy(iota[:, :], iota_i).then_inc(iota_done, 1)

            def gather(b, p):
                after(pool, pv_done, (b - 1) * HK)
                g.tensor_copy(idx[p][:, :], v_idx[:, ds(b * LC, LC)]).then_inc(idx_done, 1)
                hold(pool, idx_done, b + 1, idx_seen)
                for c in range(LC):
                    g.indirect_dma_start(out=values[p][:, c].rearrange("p h two d -> p (h two d)"),
                                         out_offset=None, in_=v_d,
                                         in_offset=bass.IndirectOffsetOnAxis(idx[p][:, c:c + 1], 0)
                                         ).then_inc(vc_in[p], 16)

            def new_tokens(n, q):
                pool.wait_ge(inv_done, n + 1)
                after(pool, tr_done, n - 1)
                g.tensor_tensor(norm[q][:, L:L + P].rearrange("p (a s) -> p a s", s=S),
                                prob[q][:, cached(q)[1]].unsqueeze(1).to_broadcast([P, 4, S]),
                                col[q][:, 3:4].unsqueeze(1).to_broadcast([P, 4, S]), ALU.mult
                                ).then_inc(new_done, 1)

            def out_low(t, k, p):
                pool.wait_ge(oh_done, t * (U // QUAD) + k + 1)
                src, dst = quad_views(k, p)
                g.tensor_tensor(dst[1], src, dst[0], ALU.subtract).then_inc(ol_done, 1)

            def body(t, p, past):
                for i in range(U):
                    if past or i:
                        new_tokens(t * U + i - 1, (i - 1) % 2)
                    if i % QUAD == 3 and (past or i > 3):
                        quad_of_step(out_low, t, i, p)
                    if i % HK == HK // 2:
                        bi = i // HK + 1
                        if bi < BT or not (isinstance(t, int) and t == NT - 1):
                            gather(t * BT + bi, bi % 2)

            gather(0, 0)
            body(0, 0, 0)
            body(1, 1, 1)
            with pool.Fori(2, NT - 3, 2) as t:
                body(t, 0, 2)
                body(t + 1, 1, 2)
            body(NT - 2, 0, 2)
            body(NT - 1, 1, 2)
            new_tokens(NT * U - 1, 1)
            out_low(NT - 1, U // QUAD - 1, 1)

        @block.tensor
        def _(pe):
            mm = nc.tensor.matmul

            def scores(t, i):
                bi, h = divmod(i, HK)
                p, q = bi % 2, i % 2
                n = t * U + i
                if h == 0:
                    pe.wait_ge(kq_in[p], (NPP + 2) * 16 * (t * (BT // 2) + bi // 2 + 1))
                after(pe, max_done, n)
                qh, ql = query[p][:, h, 0, :], query[p][:, h, 1, :]
                kh, kl = keys[p][:, 0:NPP, h, 0, :], keys[p][:, 0:NPP, h, 1, :]
                nh, nl = keys[p][:, NPP, h, 0, :], keys[p][:, NPP, h, 1, :]
                old, new = (sc[q][:, part] for part in cached(q))
                old = old.rearrange("p (n s) -> p n s", s=PS)
                for a, k, kn, start, stop in ((qh, kh, nh, True, False), (qh, kl, nl, False, False),
                                              (ql, kh, nh, False, True)):
                    mm(old, a, k, start=start, stop=stop)
                    last = mm(new, a, kn, start=start, stop=stop)
                last.then_inc(qk_done, 1)

            def turn(n, q):
                pe.wait_ge(norm_done, n + 1)
                after(pe, tl_done, n - 1)
                for c in range(LC):
                    nc.tensor.transpose(tr[q][:, c * P:(c + 1) * P], norm[q][:, c * P:(c + 1) * P], ident[:, :])
                pe.wait_ge(new_done, n + 1)
                after(pe, tl_done, n)
                nc.tensor.transpose(tr_new[:, 0:P], norm[q][:, L:L + P], ident[:, :]).then_inc(tr_done, 1)

            def weigh(t, i):
                bi, h = divmod(i, HK)
                p, q = bi % 2, i % 2
                n = t * U + i
                if h == 0:
                    pe.wait_ge(vc_in[p], LC * 16 * (t * (BT // 2) + bi // 2 + 1))
                    pe.wait_ge(vn_in[p], 16 * (t * (BT // 2) + bi // 2 + 1))
                pe.wait_ge(tl_done, n + 1)
                if i % QUAD == 0:
                    after(pe, o_kept, t * (U // QUAD) + i // QUAD)
                out = o_ps[:, (i % QUAD) * P:(i % QUAD + 1) * P]
                for c in range(LC):
                    vh, vl = values[p][:, c, h, 0, :], values[p][:, c, h, 1, :]
                    th, tl = tph[q][:, c * P:(c + 1) * P], tpl[q][:, c * P:(c + 1) * P]
                    mm(out, vh, th, start=(c == 0), stop=False)
                    mm(out, vh, tl, start=False, stop=False)
                    mm(out, vl, th, start=False, stop=False)
                mm(out, fresh[p][:, h, :], tph[q][:, L:L + P], start=False, stop=True).then_inc(pv_done, 1)

            def project(t, p, h):
                if h == 0:
                    after(pe, res_done, t)
                if h == 0 or h == HQ // 2:
                    pe.wait_ge(ol_done, (t + 1) * (U // QUAD) - (1 if h == 0 else 0))
                for a, w, start, stop in ((0, 0, True, False), (0, 1, False, False), (1, 0, False, True)):
                    last = mm(y_ps[:, :], ot[p][:, a, h, :], wo[:, h, w, :], start=(h == 0 and start),
                              stop=(h == HQ - 1 and stop))
                if h == HQ - 1:
                    last.then_inc(y_done, 1)

            def body(t, p, past):
                for i in range(U):
                    scores(t, i)
                    if past or i >= 2:
                        turn(t * U + i - 2, i % 2)
                    if past:
                        if past == 1 and i == START:
                            pe.wait_ge(wo_in, 16)
                        for h in heads_of_step(i):
                            project(t - 1, 1 - p, h)
                    if past or i >= 3:
                        weigh(*((t, i - 3) if i >= 3 else (t - 1, i - 3 + U)))

            groups(pe, body)
            for i in (U, U + 1):
                turn((NT - 1) * U + i - 2, i % 2)
                weigh(NT - 1, i - 3)
            weigh(NT - 1, U - 1)
            for h in range(HQ):
                project(NT - 1, (NT - 1) % 2, h)

        @block.scalar
        def _(act):
            copy = lambda out, in_, **kw: nc.scalar.activation(out, in_, ACT.Copy, **kw)

            def exps(n, q):
                act.wait_ge(nb_done, n + 1)
                nc.scalar.activation(prob[q][:, :], prob[q][:, :], ACT.Exp, bias=col[q][:, 1:2],
                                     scale=cs[:, 0:1], accum_out=col[q][:, 2:3]).then_inc(exp_done, 1)

            def high(n, q):
                act.wait_ge(tr_done, n + 1)
                after(act, pv_done, n - 1)
                copy(tph[q][:, 0:L], tr[q][:, :], scale=TOP)
                copy(tph[q][:, L:L + P], tr_new[:, 0:P], scale=TOP).then_inc(th_done, 1)

            def keep_out(t, k, p):
                act.wait_ge(pv_done, t * U + (k + 1) * QUAD)
                after(act, ol_done, t * (U // QUAD) + k)
                copy(of[:, :], o_ps[:, :], scale=1.0 / TOP).then_inc(o_kept, 1)

            def body(t, p, past):
                for i in range(U):
                    n = t * U + i
                    if i % QUAD == 3 and (past or i > 3):
                        quad_of_step(keep_out, t, i, p)
                    if past or i >= 2:
                        high(n - 2, i % 2)
                    exps(n, i % 2)

            groups(act, body)
            n = NT * U
            high(n - 2, 0)
            high(n - 1, 1)
            keep_out(NT - 1, U // QUAD - 1, 1)

        @block.vector
        def _(dve):
            v = nc.vector

            def make_mask(t, bi):
                b = t * BT + bi
                v.tensor_scalar(out=mask[bi % 2][:, S:S + L], in0=iota[:, :], scalar1=lens_f[:, ds(b, 1)],
                                scalar2=MASKED, op0=ALU.is_ge, op1=ALU.mult).then_inc(mask_done, 1)

            def maximum(t, i):
                bi, h = divmod(i, HK)
                q = i % 2
                n = t * U + i
                if h == 0:
                    make_mask(t, bi)
                    dve.wait_ge(mask_done, t * BT + bi + 1)
                after(dve, norm_done, n - 1)
                after(dve, new_done, n - 1)
                hold(dve, qk_done, n + 1, qk_seen)
                at = S if q == 0 else 0
                v.tensor_tensor_reduce(out=prob[q][:, :], in0=sc[q], in1=mask[bi % 2][:, at:at + LK], scale=1.0,
                                       scalar=-3.0e38, op0=ALU.add, op1=ALU.max, accum_out=col[q][:, 0:1]
                                       ).then_inc(max_done, 1)

            def negative(n, q):
                dve.wait_ge(max_done, n + 1)
                v.tensor_scalar(out=col[q][:, 1:2], in0=col[q][:, 0:1], scalar1=cs[:, 1:2], scalar2=None,
                                op0=ALU.mult).then_inc(nb_done, 1)

            def inverse(n, q):
                dve.wait_ge(exp_done, n + 1)
                v.reciprocal(col[q][:, 3:4], col[q][:, 2:3]).then_inc(inv_done, 1)

            def normalise(n, q):
                dve.wait_ge(inv_done, n + 1)
                after(dve, tr_done, n - 1)
                v.tensor_scalar(out=norm[q][:, 0:L], in0=prob[q][:, cached(q)[0]], scalar1=col[q][:, 3:4],
                                scalar2=None, op0=ALU.mult).then_inc(norm_done, 1)

            def low(n, q):
                dve.wait_ge(th_done, n + 1)
                after(dve, pv_done, n - 1)
                v.scalar_tensor_tensor(out=tpl[q][:, :], in0=tr[q][:, :], scalar=TOP, in1=tph[q][:, 0:L],
                                       op0=ALU.mult, op1=ALU.subtract)
                rows = slice(3 * S, 4 * S)
                v.scalar_tensor_tensor(out=tph[q][rows, L:L + P], in0=tr_new[rows, 0:P], scalar=TOP,
                                       in1=tph[q][rows, L:L + P], op0=ALU.mult, op1=ALU.subtract
                                       ).then_inc(tl_done, 1)

            def out_high(t, k, p):
                dve.wait_ge(o_kept, t * (U // QUAD) + k + 1)
                if k == 0:
                    after(dve, y_done, t - 1)
                src, dst = quad_views(k, p)
                v.tensor_copy(dst[0], src).then_inc(oh_done, 1)

            def result(t, p):
                dve.wait_ge(y_done, t + 1)
                dve.wait_ge(x_in[p], 8 * t + 8 * (2 - p))
                v.scalar_tensor_tensor(out=res[p][:, :], in0=y_ps[:, :], scalar=oscale[:, :], in1=res[p][:, :],
                                       op0=ALU.mult, op1=ALU.add).then_inc(res_done, 1)

            def body(t, p, past):
                for i in range(U):
                    n = t * U + i
                    maximum(t, i)
                    if past or i >= 1:
                        inverse(n - 1, (i - 1) % 2)
                    negative(n, i % 2)
                    if past or i >= 1:
                        normalise(n - 1, (i - 1) % 2)
                    if past or i >= 2:
                        low(n - 2, i % 2)
                    if i == 0 and past == 2:
                        result(t - 2, p)
                    if i % QUAD == 3 and (past or i > 3):
                        quad_of_step(out_high, t, i, p)

            v.memset(mask[0][:, :], 0.0).then_inc(unmasked, 1)
            v.memset(mask[1][:, :], 0.0).then_inc(unmasked, 1)
            dve.wait_ge(unmasked, 2)
            dve.wait_ge(iota_done, 1)
            groups(dve, body)
            n = NT * U
            inverse(n - 1, 1)
            normalise(n - 1, 1)
            low(n - 2, 0)
            result(NT - 2, 0)
            low(n - 1, 1)
            out_high(NT - 1, U // QUAD - 1, 1)
            result(NT - 1, 1)


def kernel(x, itok_B_0_15, itok_B_0_7, itok_Bx16_0_63, itok_B_207_1644, L0_cond_weights, L1_cond_W, L1_cond_Wr,
           L1_cond_A, L1_cond_B, L2_cond_weights, L3_cond_Wq, L3_cond_Wk, L3_cond_Wv, L3_cond_Wo,
           L3_cond_q_norm_w, L3_cond_k_norm_w, L3_cond_k_cache, L3_cond_v_cache):
    import numpy as np
    import concourse.bacc as bacc
    from concourse.bass_utils import run_bass_kernel_spmd

    def per_group(a):
        return np.asarray(a).reshape(NT, BT).T

    power = np.float32(10000.0) ** (np.arange(0, HD, 2, dtype=np.float32) / np.float32(HD))
    laid_out = [
        ("x", x),
        ("cond_r", per_group(itok_B_0_15)),
        ("lang_r", per_group(itok_B_0_7)),
        ("len_r", per_group(itok_B_207_1644)),
        ("lens", itok_B_207_1644),
        ("pages", itok_Bx16_0_63),
        ("pages_r", np.asarray(itok_Bx16_0_63).reshape(B * LC, BT).T),
        ("mix0", np.asarray(L0_cond_weights).reshape(SETS * S, MIX)),
        ("mix2", np.asarray(L2_cond_weights).reshape(SETS * S, MIX)),
        ("lin_t", np.asarray(L1_cond_W).T),
        ("router_t", np.asarray(L1_cond_Wr).T),
        ("a_t", np.asarray(L1_cond_A).reshape(ER, D).T),
        ("b_t", np.asarray(L1_cond_B).transpose(0, 2, 1).reshape(ER, D)),
        ("wq_t", np.asarray(L3_cond_Wq).T),
        ("wk_t", np.asarray(L3_cond_Wk).T),
        ("wv_t", np.asarray(L3_cond_Wv).T),
        ("wo_t", np.asarray(L3_cond_Wo).T),
        ("q_norm", L3_cond_q_norm_w),
        ("k_norm", L3_cond_k_norm_w),
        ("k_t", np.asarray(L3_cond_k_cache).transpose(0, 3, 2, 1).reshape(PAGES, P, HK * PS)),
        ("v_rows", np.asarray(L3_cond_v_cache).reshape(PAGES * PS, NKV)),
        ("inv_freq", (np.float32(1.0) / power).astype(np.float32)),
    ]
    nc = bacc.Bacc("TRN2", target_bir_lowering=False, num_devices=1)
    arrays, args = {}, []
    for name, a in laid_out:
        a = np.ascontiguousarray(a)
        arrays["in_" + name] = a
        args.append(nc.dram_tensor("in_" + name, a.shape, mybir.dt.from_np(a.dtype), kind="ExternalInput").ap())
    args.append(nc.dram_tensor("out_0", (B, S, D), F32, kind="ExternalOutput").ap())
    conditional_residual(nc, *args)
    got = run_bass_kernel_spmd(nc, [arrays], core_ids=[0])
    return got.results[0]["out_0"]
```

```python
from contextlib import ExitStack

import concourse.bass as bass
from concourse import mybir
from concourse.alu_op_type import AluOpType as ALU

F32, F16, BF16 = mybir.dt.float32, mybir.dt.float16, mybir.dt.bfloat16
I32, U32 = mybir.dt.int32, mybir.dt.uint32
ACT = mybir.ActivationFunctionType
AX = mybir.AxisListType
SP = mybir.EngineType.SP
RMAX = bass.bass_isa.ReduceOp.max
ds = bass.ds

P = 128
B, S, D = 64, 32, 512
BT = P // S
NT = B // BT
KD = D // P
SETS, MIX = 16, 32
E, R = 8, 16
ER = E * R
ROUTE = E + ER
HD, HQ, HK = 128, 32, 8
REP = HQ // HK
PAGES, PS, NPP = 64, 32, 16
L = PS * NPP
LK = L + S
LC = L // P
NQ, NKV = HQ * HD, HK * HD
NW = NQ + 2 * NKV
QB, KB, VB = NQ // D, NKV // D, NKV // D
ROT = QB + KB
BLK = ROT + VB
HB = D // HD
HALF = HD // 2
HALVES = ROT * HB
PG = HK * 2 * PS
EPS = 1e-6
SCALE = float(HD) ** -0.5
TOP = 2.0 ** 14
TINY = 2.0 ** -16
EXPONENT = 0x7F800000
MASKED = -1e30
LANG_BIAS, LORA = 5.0, 32.0 / 16.0
ROUND = 1.5 * 2.0 ** 23
TWO_PI = (6.28125, 0.0019350051879882812, 3.019916050561733e-07)
TI = 4
NG = NT // TI
CH = 2048
WC = 1024
WN = NW // WC
SC = 512
SCAN = 2


def after(eng, sem, value):
    if not isinstance(value, int) or value > 0:
        eng.wait_ge(sem, value)


def hold(eng, sem, value, passed):
    eng.wait_ge(sem, value)
    eng.sem_inc(passed, 1)


def scales_of(v, step, mag, pow2, up, down, cols):
    step(v.tensor_scalar(out=mag[:, cols], in0=mag[:, cols], scalar1=TINY, scalar2=None, op0=ALU.max))
    step(v.tensor_scalar(out=pow2[:, cols].bitcast(I32), in0=mag[:, cols].bitcast(I32), scalar1=EXPONENT,
                         scalar2=None, op0=ALU.bitwise_and))
    step(v.reciprocal(up[:, cols], pow2[:, cols]))
    step(v.tensor_scalar(out=up[:, cols], in0=up[:, cols], scalar1=TOP, scalar2=None, op0=ALU.mult))
    step(v.tensor_scalar(out=down[:, cols], in0=pow2[:, cols], scalar1=1.0 / TOP, scalar2=None, op0=ALU.mult))


def conditional_residual(nc, x, per_row, lens, pages, mixers, lin_t, route_t, b_t, w_t, wo_t, q_norm, k_norm,
                         k_t, v_rows, inv_freq, out):
    x_v = x.rearrange("(t b) s d -> t (b s) d", b=BT)
    out_v = out.rearrange("(t b) s d -> t (b s) d", b=BT)
    x3_d = nc.dram_tensor("x3_scratch", (NT, P, D), F32).ap()
    k_d = nc.dram_tensor("k_parts", (PAGES, P, PG), F16).ap()
    v_d = nc.dram_tensor("v_parts", (PAGES * PS, HK * 2 * HD), F16).ap()
    wo_d = nc.dram_tensor("wo_parts", (P, HQ, 2, D), F16).ap()
    kn_d = nc.dram_tensor("k_new_parts", (B, P, PG), F16).ap()
    vn_d = nc.dram_tensor("v_new_parts", (BT, B * S, NKV), BF16).ap()
    q_d = nc.dram_tensor("q_parts", (NT, QB, P, BT, 2 * HB * S), F16).ap()

    whole = ExitStack()
    with whole:
        def keep(name, shape, dt):
            return whole.enter_context(nc.sbuf_tensor(name, shape, dt))

        ident = keep("ident", [P, P], F32)
        ident16 = keep("ident16", [P, P], F16)
        mag = keep("mag", [P, 5], F32)
        pow2 = keep("pow2", [P, 5], F32)
        up = keep("up", [P, 5], F32)
        down = keep("down", [P, 5], F32)
        cs = keep("cs", [P, 2], F32)
        vw = keep("vw", [P, 1], F32)
        oscale = keep("oscale", [P, 1], F32)
        v_idx = keep("v_idx", [P, B * LC], I32)
        lens_f = keep("lens_f", [P, B], F32)

        ab = ExitStack()
        with ab:
            def mid(name, shape, dt):
                return ab.enter_context(nc.sbuf_tensor(name, shape, dt))

            place = mid("place", [P, NT], F32)
            freq = mid("freq", [P, HALF], F32)
            cos = mid("cos", [P, NT, HALF], F32)
            sin = mid("sin", [P, NT, HALF], F32)
            wa = mid("wa", [P, 2, HD], F32)
            wb = mid("wb", [P, 2, HD], F32)
            wh = mid("wh", [P, KD, NW], F16)
            wl = mid("wl", [P, KD, NW], F16)
            with ExitStack() as mix:
                mt = lambda name, shape, dt: mix.enter_context(nc.sbuf_tensor(name, shape, dt))
                blocks = mt("blocks", [P, BT, S], F32)
                mixer = mt("mixer", [P, NT, 2, MIX], F32)
                bias = mt("bias", [P, NT, E], F32)
                iota8 = mt("iota8", [P, E], F32)
                lin = mt("lin", [P, KD, D], F32)
                route = mt("route", [P, KD, ROUTE], F32)
                low = mt("low", [ER, D], F32)
                xa = [mt(f"xa{j}", [P, D], F32) for j in range(TI)]
                prologue(nc, ident, ident16, mag, pow2, up, down, v_idx, lens_f, place, freq, wa, blocks, mixer, bias,
                         iota8, lin, route, low, xa, per_row, lens, mixers, lin_t, route_t, b_t, w_t, x_v, q_norm,
                         k_norm, inv_freq)
                mixing(nc, ident, mag, pow2, up, down, cs, vw, oscale, wa, wb, wh, wl, blocks, mixer, bias, iota8,
                       lin, route, low, xa, x_v, w_t, wo_t, k_t, v_rows, x3_d)
            projections(nc, ident, ident16, up, vw, place, freq, cos, sin, wa, wb, wh, wl, wo_t, k_t, v_rows, x3_d, q_d, kn_d,
                        vn_d, k_d, v_d, wo_d)
        attention(nc, ident, cs, oscale, v_idx, lens_f, pages, k_d, v_d, kn_d, vn_d, q_d, wo_d, x3_d, out_v)


def prologue(nc, ident, ident16, mag, pow2, up, down, v_idx, lens_f, place, freq, wa, blocks, mixer, bias, iota8,
             lin, route, low, xa, per_row, lens, mixers, lin_t, route_t, b_t, w_t, x_v, q_norm, k_norm, inv_freq):
    ctx = ExitStack()
    with ctx:
        def sb(name, shape, dt):
            return ctx.enter_context(nc.sbuf_tensor("pro_" + name, shape, dt))

        def sem(name):
            return ctx.enter_context(nc.semaphore("pro_" + name))

        sources = [w_t[k * P:(k + 1) * P, c:c + CH] for k in range(KD) for c in range(0, NW, CH)]
        NBUF = 4
        ring = sb("ring", [P, NBUF, CH], F32)
        found = sb("found", [P, len(sources)], F32)
        per_i = sb("per_i", [P, 3 * NT + B * LC], I32)
        cond_i, lang_i, len_i = (per_i[:, i * NT:(i + 1) * NT] for i in range(3))
        pages_i = per_i[:, 3 * NT:3 * NT + B * LC]
        lens_i = sb("lens_i", [P, B], I32)
        small = sb("small", [P, 4, NT], F32)
        row_i = sb("row_i", [P, 1], I32)
        row_f = sb("row_f", [P, 1], F32)
        mix_idx = sb("mix_idx", [P, NT], U32)
        mix_col = sb("mix_col", [P, NT], F32)
        pages_f = sb("pages_f", [P, B * LC], F32)
        iota_i = sb("iota_i", [P, E], I32)
        loaded = [sem(f"loaded{i}") for i in range(NBUF)]
        scanned, inputs, made, gathered = sem("scanned"), sem("inputs"), sem("made"), sem("gathered")
        chain, reduced, ready, local = sem("chain"), sem("reduced"), sem("index_ready"), sem("local")
        pool_chain, kept = sem("pool_chain"), sem("kept")

        block = ctx.enter_context(nc.Block())
        N_IN = BT + 1 + 2 + 1

        @block.sync
        def _(sp):
            for r in range(BT):
                rows = slice(r * S, (r + 1) * S)
                sp.dma_start(per_i[rows, :], per_row[r:r + 1, :].to_broadcast([S, per_row.shape[1]])
                             ).then_inc(inputs, 16)
            sp.dma_start(lens_i[:, :], lens.rearrange("(o b) -> o b", o=1).to_broadcast([P, B])).then_inc(inputs, 16)
            for i, w in enumerate((q_norm, k_norm)):
                sp.dma_start(wa[:, i, :], w.rearrange("(o d) -> o d", o=1).to_broadcast([P, HD])).then_inc(inputs, 16)
            sp.dma_start(freq[:, :], inv_freq.rearrange("(o d) -> o d", o=1).to_broadcast([P, HALF])).then_inc(inputs, 16)
            sp.dma_start(lin[:, :, :], lin_t.rearrange("(k p) o -> p k o", p=P)).then_inc(kept, 16)
            sp.dma_start(route[:, :, :], route_t.rearrange("(k p) e -> p k e", p=P)).then_inc(kept, 16)
            sp.dma_start(low[:, :], b_t).then_inc(kept, 16)
            for j in range(TI):
                sp.dma_start(xa[j][:, :], x_v[j]).then_inc(kept, 16)
            for i, src in enumerate(sources):
                after(sp, scanned, i - NBUF + 1)
                sp.dma_start(ring[:, i % NBUF, :], src).then_inc(loaded[i % NBUF], 16)
            sp.wait_ge(kept, (3 + TI) * 16)

        @block.gpsimd
        def _(pool):
            n = 0

            def step(ins):
                nonlocal n
                n += 1
                ins.then_inc(pool_chain, 1)
                pool.wait_ge(pool_chain, n)

            step(nc.gpsimd.memset(ident[:, :], 0.0))
            step(nc.gpsimd.affine_select(out=ident[:, :], in_=ident[:, :], compare_op=ALU.not_equal, fill=1.0,
                                         base=0, pattern=[[-1, P]], channel_multiplier=1))
            step(nc.gpsimd.tensor_copy(ident16[:, :], ident[:, :]))
            step(nc.gpsimd.memset(blocks[:, :, :], 1.0))
            step(nc.gpsimd.affine_select(out=blocks[:, :, :], in_=blocks[:, :, :], compare_op=ALU.is_ge, fill=0.0,
                                         base=0, pattern=[[-S, BT], [0, S]], channel_multiplier=1))
            step(nc.gpsimd.affine_select(out=blocks[:, :, :], in_=blocks[:, :, :], compare_op=ALU.is_ge, fill=0.0,
                                         base=S - 1, pattern=[[S, BT], [0, S]], channel_multiplier=-1))
            step(nc.gpsimd.iota(iota_i[:, :], pattern=[[1, E]], base=0, channel_multiplier=0))
            step(nc.gpsimd.tensor_copy(iota8[:, :], iota_i[:, :]))
            step(nc.gpsimd.iota(row_i[:, :], pattern=[[0, 1]], base=0, channel_multiplier=1))
            nc.gpsimd.tensor_copy(row_f[:, :], row_i[:, :]).then_inc(made, 1)
            pool.wait_ge(ready, 1)
            for t in range(NT):
                nc.gpsimd.indirect_dma_start(out=mixer[:, t].rearrange("p a d -> p (a d)"), out_offset=None,
                                             in_=mixers,
                                             in_offset=bass.IndirectOffsetOnAxis(mix_idx[:, t:t + 1], 0)
                                             ).then_inc(gathered, 16)
            pool.wait_ge(local, 1)
            nc.gpsimd.partition_all_reduce(mag[:, 3:4], pow2[:, 3:4], P, RMAX).then_inc(reduced, 1)
            pool.wait_ge(gathered, NT * 16)

        @block.vector
        def _(dve):
            n = 0

            def step(ins):
                nonlocal n
                n += 1
                ins.then_inc(chain, 1)
                dve.wait_ge(chain, n)

            v = nc.vector
            dve.wait_ge(inputs, N_IN * 16)
            dve.wait_ge(made, 1)
            step(v.tensor_copy(small[:, 0, :], cond_i))
            step(v.tensor_copy(small[:, 1, :], len_i))
            step(v.tensor_copy(small[:, 2, :], lang_i))
            step(v.tensor_copy(lens_f[:, :], lens_i[:, :]))
            step(v.tensor_copy(pages_f[:, :], pages_i))
            step(v.tensor_scalar(out=small[:, 3, 0:1], in0=row_f[:, :], scalar1=float(S), scalar2=-float(S),
                                 op0=ALU.is_ge, op1=ALU.mult))
            for r in range(2, BT):
                step(v.tensor_scalar(out=small[:, 3, r:r + 1], in0=row_f[:, :], scalar1=float(r * S),
                                     scalar2=-float(S), op0=ALU.is_ge, op1=ALU.mult))
                step(v.tensor_tensor(small[:, 3, 0:1], small[:, 3, 0:1], small[:, 3, r:r + 1], ALU.add))
            step(v.tensor_tensor(small[:, 3, 1:2], small[:, 3, 0:1], row_f[:, :], ALU.add))
            within = small[:, 3, 1:2]
            step(v.tensor_scalar(out=mix_col[:, :], in0=small[:, 0, :], scalar1=float(MIX), scalar2=within,
                                 op0=ALU.mult, op1=ALU.add))
            v.tensor_copy(mix_idx[:, :], mix_col[:, :]).then_inc(ready, 1)
            step(v.tensor_scalar(out=pages_f[:, :], in0=pages_f[:, :], scalar1=float(PS), scalar2=within,
                                 op0=ALU.mult, op1=ALU.add))
            step(v.tensor_copy(v_idx[:, :], pages_f[:, :]))
            for t in range(NT):
                last = v.tensor_scalar(out=bias[:, t, :], in0=iota8[:, :], scalar1=small[:, 2, t:t + 1],
                                       scalar2=LANG_BIAS, op0=ALU.is_equal, op1=ALU.mult)
            step(last)
            step(v.tensor_scalar(out=place[:, :], in0=small[:, 1, :], scalar1=within, scalar2=None, op0=ALU.add))
            for i in range(len(sources)):
                dve.wait_ge(loaded[i % NBUF], 16 * (i // NBUF + 1))
                v.tensor_reduce(found[:, i:i + 1], ring[:, i % NBUF, :], AX.X, ALU.max,
                                apply_absolute_value=True).then_inc(scanned, 1)
            dve.wait_ge(scanned, len(sources))
            v.tensor_reduce(pow2[:, 3:4], found[:, :], AX.X, ALU.max).then_inc(local, 1)
            step(v.tensor_reduce(pow2[:, 4:5], wa[:, 0, :], AX.X, ALU.max, apply_absolute_value=True))
            step(v.tensor_scalar(out=mag[:, 4:5], in0=pow2[:, 4:5], scalar1=16.0, scalar2=None, op0=ALU.mult))
            dve.wait_ge(reduced, 1)
            scales_of(v, step, mag, pow2, up, down, slice(3, 5))


def mixing(nc, ident, mag, pow2, up, down, cs, vw, oscale, wa, wb, wh, wl, blocks, mixer, bias, iota8, lin,
           route, low, xa, x_v, w_t, wo_t, k_t, v_rows, x3_d):
    ctx = ExitStack()
    with ctx:
        def sb(name, shape, dt):
            return ctx.enter_context(nc.sbuf_tensor("mix_" + name, shape, dt))

        def sem(name):
            return ctx.enter_context(nc.semaphore("mix_" + name))

        xb = [sb(f"xb{j}", [P, D], F32) for j in range(TI)]
        xc = [sb(f"xc{j}", [P, D], F32) for j in range(TI)]
        m0 = [sb(f"m0{j}", [P, BT, MIX], F32) for j in range(TI)]
        m2 = [sb(f"m2{j}", [P, BT, MIX], F32) for j in range(TI)]
        x1t = [sb(f"x1t{j}", [P, D], F32) for j in range(TI)]
        logit = [sb(f"logit{j}", [P, E], F32) for j in range(TI)]
        top = [sb(f"top{j}", [P, 8], F32) for j in range(TI)]
        top_i = [sb(f"top_i{j}", [P, 8], U32) for j in range(TI)]
        top_f = [sb(f"top_f{j}", [P, 8], F32) for j in range(TI)]
        gate = [sb(f"gate{j}", [P, 3, E], F32) for j in range(TI)]
        w = [sb(f"w{j}", [P, 8], F32) for j in range(TI)]
        hg = [sb(f"hg{j}", [P, ER], F32) for j in range(TI)]
        hgt = [sb(f"hgt{j}", [P, P], F32) for j in range(TI)]
        wraw = [sb(f"wraw{i}", [P, 1, WC], F32) for i in range(3)]
        ring = [sb(f"ring{i}", [P, CH], F32) for i in range(2)]
        found = sb("found", [P, 3, SCAN * NG], F32)
        kmax = sb("kmax", [P, 1], F32)
        ps = [ctx.enter_context(nc.psum_tensor(f"mix_ps{j}", [P, D], F32)) for j in range(TI)]
        base = [ctx.enter_context(nc.psum_tensor(f"mix_base{j}", [P, D], F32)) for j in range(TI)]

        chain, passed = sem("chain"), sem("passed")
        xin = [sem(f"xin{j}") for j in range(TI)]
        matrices, first, one, turned, one_t, lin_done = (sem(s) for s in (
            "matrices", "first", "x1", "x1_turned", "x1t", "lin"))
        w_seen = sem("weights_seen")
        margin, shares, gated, h_turned, hg_t, experts, two, last_mix, three = (sem(s) for s in (
            "margin", "shares", "gated", "h_turned", "hgt", "experts", "x2", "last_mix", "x3"))
        stored = [sem(f"stored{j}") for j in range(TI)]

        routed, last_chain, reduced, local = (sem(s) for s in ("routed", "scales", "reduced", "local"))
        w_loaded = [sem(f"weights_in{i}") for i in range(3)]
        ring_in = [sem(f"ring_in{i}") for i in range(2)]
        w_high, w_scaled, w_low, w_passed, scanned = (sem(s) for s in (
            "weights_high", "weights_scaled", "weights_low", "weights_passed", "scanned"))
        w_src = w_t.rearrange("(k p) (c m) -> k c p m", p=P, m=WC)
        sources = (k_t.rearrange("(c n) p m -> c p n m", n=CH // (HK * PS)),
                   v_rows.rearrange("(c n p) m -> c p n m", p=P, n=CH // NKV),
                   wo_t.rearrange("(c n p) m -> c p n m", p=P, n=CH // D))

        def load_scan(sp, g, s):
            src = sources[s // SCAN][ds(g * SCAN + s % SCAN, 1)].rearrange("o p n m -> (o p) n m")
            sp.dma_start(ring[s % 2][:, :].rearrange("p (n m) -> p n m", m=src.shape[2]), src
                         ).then_inc(ring_in[s % 2], 16)

        NS = 3 * SCAN
        block = ctx.enter_context(nc.Block())

        @block.sync
        def _(sp):
            for s in range(2):
                load_scan(sp, 0, s)

            def scans(g):
                for s in range(NS):
                    last_group = isinstance(g, int)
                    if s + 2 < NS or not last_group:
                        sp.wait_ge(scanned, g * NS + s + 1)
                        load_scan(sp, *((g, s + 2) if s + 2 < NS else (g + 1, s + 2 - NS)))

            def store(t, j):
                sp.wait_ge(three, t + j + 1)
                sp.dma_start(x3_d[ds(t + j, 1)].rearrange("o p d -> (o p) d"), xc[j][:, :]).then_inc(stored[j], 16)

            with sp.Fori(0, NG - 1) as g:
                t = g * TI
                for j in range(TI):
                    sp.wait_ge(one, t + j + 1)
                    sp.dma_start(xa[j][:, :], x_v[ds(t + TI + j, 1)].rearrange("o p d -> (o p) d")
                                 ).then_inc(xin[j], 16)
                scans(g)
                for j in range(TI):
                    store(t, j)
            scans(NG - 1)
            for j in range(TI):
                store(NT - TI, j)
            for j in range(TI):
                sp.wait_ge(stored[j], 16 * (NG + 1))

        @block.scalar
        def _(act):
            def split(g, c):
                n = g * WN + c
                buf = wraw[c % 3]
                hold(act, w_loaded[c % 3], 16 * (g * (WN // 3) + c // 3 + 1), w_passed)
                nc.scalar.activation(wh[:, ds(g, 1), c * WC:(c + 1) * WC], buf[:, :, :], ACT.Copy,
                                     scale=up[:, 3:4]).then_inc(w_high, 1)
                act.wait_ge(w_high, n + 1)
                nc.scalar.activation(buf[:, :, :], buf[:, :, :], ACT.Copy, scale=up[:, 3:4]).then_inc(w_scaled, 1)

            with act.Fori(0, NG) as g:
                t = g * TI
                for j in range(TI):
                    act.wait_ge(turned, t + j + 1)
                    nc.scalar.activation(x1t[j][:, :], ps[j][:, :], ACT.Copy).then_inc(one_t, 1)
                for c in range(2):
                    split(g, c)
                for j in range(TI):
                    act.wait_ge(margin, t + j + 1)
                    nc.scalar.activation(w[j][:, 1:2], w[j][:, 0:1], ACT.Exp).then_inc(shares, 1)
                split(g, 2)
                for j in range(TI):
                    act.wait_ge(h_turned, t + j + 1)
                    nc.scalar.activation(hgt[j][:, :], ps[j][:, 0:P], ACT.Copy).then_inc(hg_t, 1)
                for c in range(3, WN):
                    split(g, c)

        @block.gpsimd
        def _(pool):
            def load(g, c):
                pool.dma_start(wraw[c % 3][:, 0, :], w_src[ds(g, 1), c].rearrange("o p m -> (o p) m")
                               ).then_inc(w_loaded[c % 3], 16)

            def low_parts(g):
                for c in range(WN):
                    n = g * WN + c
                    out = wl[:, ds(g, 1), c * WC:(c + 1) * WC]
                    hold(pool, w_scaled, n + 1, w_seen)
                    nc.gpsimd.tensor_tensor(out, wraw[c % 3][:, :, :], wh[:, ds(g, 1), c * WC:(c + 1) * WC],
                                            ALU.subtract).then_inc(w_low, 1)
                    if c + 3 < WN or not isinstance(g, int):
                        hold(pool, w_low, n + 1, w_seen)
                        load(*((g, c + 3) if c + 3 < WN else (g + 1, c + 3 - WN)))

            for c in range(3):
                load(0, c)
            with pool.Fori(0, NG - 1) as g:
                low_parts(g)
            low_parts(NG - 1)
            pool.wait_ge(local, 1)
            nc.gpsimd.partition_all_reduce(mag[:, 0:3], pow2[:, 0:3], P, RMAX).then_inc(reduced, 1)

        @block.tensor
        def _(pe):
            mm = nc.tensor.matmul
            with pe.Fori(0, NG) as g:
                t = g * TI
                for j in range(TI):
                    pe.wait_ge(xin[j], 16 * g + 16)
                    pe.wait_ge(matrices, t + j + 1)
                    mm(ps[j][:, :], m0[j][:, :, :].rearrange("p b d -> p (b d)"), xa[j][:, :], start=True,
                       stop=True).then_inc(first, 1)
                for j in range(TI):
                    pe.wait_ge(one, t + j + 1)
                    for k in range(KD):
                        last = nc.tensor.transpose(ps[j][:, k * P:(k + 1) * P], xb[j][:, k * P:(k + 1) * P],
                                                   ident[:, :])
                    last.then_inc(turned, 1)
                for j in range(TI):
                    pe.wait_ge(one_t, t + j + 1)
                    for k in range(KD):
                        last = mm(ps[j][:, 0:ROUTE], x1t[j][:, k * P:(k + 1) * P], route[:, k, :], start=(k == 0),
                                  stop=(k == KD - 1))
                    last.then_inc(routed, 1)
                for j in range(TI):
                    for k in range(KD):
                        last = mm(base[j][:, :], x1t[j][:, k * P:(k + 1) * P], lin[:, k, :], start=(k == 0),
                                  stop=False)
                last.then_inc(lin_done, 1)
                for j in range(TI):
                    pe.wait_ge(gated, t + j + 1)
                    nc.tensor.transpose(ps[j][:, 0:P], hg[j][:, :], ident[:, :]).then_inc(h_turned, 1)
                for j in range(TI):
                    pe.wait_ge(hg_t, t + j + 1)
                    mm(base[j][:, :], hgt[j][:, :], low[:, :], start=False, stop=True).then_inc(experts, 1)
                for j in range(TI):
                    pe.wait_ge(two, t + j + 1)
                    mm(ps[j][:, :], m2[j][:, :, :].rearrange("p b d -> p (b d)"), xc[j][:, :], start=True,
                       stop=True).then_inc(last_mix, 1)

        STEPS = 14

        @block.vector
        def _(dve):
            v = nc.vector
            for j in range(TI):
                dve.sem_inc(stored[j], 16)
                dve.sem_inc(xin[j], 16)
            with dve.Fori(0, NG) as g:
                t = g * TI
                n = [0]

                def scan(s):
                    hold(dve, ring_in[s % 2], 16 * (g * (NS // 2) + s // 2 + 1), passed)
                    v.tensor_reduce(found[:, s // SCAN, ds(g * SCAN + s % SCAN, 1)], ring[s % 2][:, :], AX.X,
                                    ALU.max, apply_absolute_value=True).then_inc(scanned, 1)

                def step(op, alone=False):
                    for j in range(TI):
                        if alone:
                            hold(dve, chain, t * STEPS + (n[0] - 1) * TI + j + 1, passed)
                        else:
                            dve.wait_ge(chain, t * STEPS + (n[0] - 1) * TI + j + 1)
                        op(j).then_inc(chain, 1)
                    n[0] += 1

                for j in range(TI):
                    for i, m in enumerate((m0, m2)):
                        last = v.tensor_tensor(m[j][:, :, :], mixer[:, ds(t + j, 1), i, :].to_broadcast([P, BT, MIX]),
                                               blocks[:, :, :], ALU.mult)
                    last.then_inc(matrices, 1)
                for j in range(TI):
                    dve.wait_ge(first, t + j + 1)
                    v.tensor_tensor(xb[j][:, :], ps[j][:, :], xa[j][:, :], ALU.add).then_inc(one, 1)
                for s in range(SCAN):
                    scan(s)
                for j in range(TI):
                    dve.wait_ge(routed, t + j + 1)
                    v.tensor_tensor(logit[j][:, :], ps[j][:, 0:E], bias[:, ds(t + j, 1), :].rearrange(
                        "p o e -> p (o e)"), ALU.add).then_inc(chain, 1)
                n[0] = 1
                step(lambda j: v.max(top[j][:, :], logit[j][:, :]), alone=True)
                step(lambda j: v.max_index(top_i[j][:, :], top[j][:, :], logit[j][:, :]), alone=True)
                scan(2)
                step(lambda j: v.tensor_copy(top_f[j][:, 0:2], top_i[j][:, 0:2]))
                step(lambda j: v.tensor_scalar(out=gate[j][:, 0, :], in0=iota8[:, :], scalar1=top_f[j][:, 0:1],
                                               scalar2=None, op0=ALU.is_equal))
                step(lambda j: v.tensor_scalar(out=gate[j][:, 1, :], in0=iota8[:, :], scalar1=top_f[j][:, 1:2],
                                               scalar2=None, op0=ALU.is_equal))
                step(lambda j: v.tensor_tensor(w[j][:, 0:1], top[j][:, 1:2], top[j][:, 0:1], ALU.subtract))
                for j in range(TI):
                    dve.wait_ge(chain, t * STEPS + (n[0] - 1) * TI + j + 1)
                    v.tensor_copy(w[j][:, 6:7], w[j][:, 0:1]).then_inc(margin, 1)
                for j in range(TI):
                    dve.wait_ge(shares, t + j + 1)
                    v.tensor_scalar(out=w[j][:, 2:3], in0=w[j][:, 1:2], scalar1=1.0, scalar2=None,
                                    op0=ALU.add).then_inc(chain, 1)
                n[0] += 1
                step(lambda j: v.reciprocal(w[j][:, 3:4], w[j][:, 2:3]))
                step(lambda j: v.tensor_scalar(out=w[j][:, 4:5], in0=w[j][:, 3:4], scalar1=LORA, scalar2=None,
                                               op0=ALU.mult))
                step(lambda j: v.tensor_tensor(w[j][:, 5:6], w[j][:, 4:5], w[j][:, 1:2], ALU.mult))
                step(lambda j: v.tensor_scalar(out=gate[j][:, 1, :], in0=gate[j][:, 1, :], scalar1=w[j][:, 5:6],
                                               scalar2=None, op0=ALU.mult))
                step(lambda j: v.scalar_tensor_tensor(out=gate[j][:, 2, :], in0=gate[j][:, 0, :],
                                                      scalar=w[j][:, 4:5], in1=gate[j][:, 1, :], op0=ALU.mult,
                                                      op1=ALU.add))
                step(lambda j: v.tensor_tensor(hg[j][:, :].rearrange("p (e r) -> p e r", r=R),
                                               ps[j][:, E:ROUTE].rearrange("p (e r) -> p e r", r=R),
                                               gate[j][:, 2, :].unsqueeze(2).to_broadcast([P, E, R]), ALU.mult))
                assert n[0] == STEPS
                for j in range(TI):
                    dve.wait_ge(chain, t * STEPS + (STEPS - 1) * TI + j + 1)
                    dve.sem_inc(gated, 1)
                for s in (3, 4):
                    scan(s)
                for j in range(TI):
                    dve.wait_ge(experts, t + j + 1)
                    dve.wait_ge(stored[j], 16 * g + 16)
                    v.tensor_tensor(xc[j][:, :], base[j][:, :], xb[j][:, :], ALU.add).then_inc(two, 1)
                for j in range(TI):
                    dve.wait_ge(last_mix, t + j + 1)
                    v.tensor_tensor(xc[j][:, :], ps[j][:, :], xc[j][:, :], ALU.add).then_inc(three, 1)
                scan(5)
            n = [0]

            def small(ins):
                n[0] += 1
                ins.then_inc(last_chain, 1)
                dve.wait_ge(last_chain, n[0])

            dve.wait_ge(scanned, NG * NS)
            for i in range(3):
                small(v.tensor_reduce(pow2[:, i:i + 1], found[:, i, :], AX.X, ALU.max))
            small(v.tensor_reduce(kmax[:, :], wa[:, 1, :], AX.X, ALU.max, apply_absolute_value=True))
            small(v.tensor_scalar(out=kmax[:, :], in0=kmax[:, :], scalar1=16.0, scalar2=None, op0=ALU.mult))
            v.tensor_tensor(pow2[:, 0:1], pow2[:, 0:1], kmax[:, :], ALU.max).then_inc(local, 1)
            dve.wait_ge(reduced, 1)
            scales_of(v, small, mag, pow2, up, down, slice(0, 3))
            small(v.tensor_tensor(cs[:, 0:1], down[:, 0:1], down[:, 4:5], ALU.mult))
            small(v.tensor_scalar(out=cs[:, 0:1], in0=cs[:, 0:1], scalar1=SCALE, scalar2=None, op0=ALU.mult))
            small(v.tensor_scalar(out=cs[:, 1:2], in0=cs[:, 0:1], scalar1=-1.0, scalar2=None, op0=ALU.mult))
            small(v.tensor_tensor(vw[:, :], up[:, 1:2], down[:, 3:4], ALU.mult))
            small(v.tensor_tensor(oscale[:, :], down[:, 1:2], down[:, 2:3], ALU.mult))
            for i, col in enumerate((4, 0)):
                small(v.tensor_scalar(out=wa[:, i, :], in0=wa[:, i, :], scalar1=up[:, col:col + 1], scalar2=None,
                                      op0=ALU.mult))
                small(v.tensor_scalar(out=wb[:, i, 0:HALF], in0=wa[:, i, HALF:HD], scalar1=-1.0, scalar2=None,
                                      op0=ALU.mult))
                small(v.tensor_copy(wb[:, i, HALF:HD], wa[:, i, 0:HALF]))


def projections(nc, ident, ident16, up, vw, place, freq, cos, sin, wa, wb, wh, wl, wo_t, k_t, v_rows, x3_d, q_d,
                kn_d, vn_d, k_d, v_d, wo_d):
    ctx = ExitStack()
    with ctx:
        def sb(name, shape, dt):
            return ctx.enter_context(nc.sbuf_tensor("proj_" + name, shape, dt))

        def sem(name):
            return ctx.enter_context(nc.semaphore("proj_" + name))

        x3 = [sb(f"x3{i}", [P, D], F32) for i in range(2)]
        col = [sb(f"col{i}", [P, 12], F32) for i in range(2)]
        xh = sb("xh", [P, D], F16)
        xl = sb("xl", [P, D], F16)
        xt = [sb(f"xt{i}", [P, KD, 2, P], F16) for i in range(2)]
        raw = [sb(f"raw{i}", [P, ROT, D], F32) for i in range(2)]
        sq = [sb(f"sq{i}", [P, D], F32) for i in range(2)]
        ss = sb("ss", [P, 4, HALVES], F32)
        inv = [sb(f"inv{i}", [P, HALVES], F32) for i in range(2)]
        ta = sb("ta", [P, 2, HD], F32)
        tb = sb("tb", [P, 2, HD], F32)
        ra = [sb(f"ra{i}", [P, D], F32) for i in range(2)]
        rb = [sb(f"rb{i}", [P, D], F32) for i in range(2)]
        rn = [sb(f"rn{i}", [P, D], F32) for i in range(2)]
        turned = [sb(f"turned{i}", [P, 2 * D], F16) for i in range(2)]
        v32 = [sb(f"v32{i}", [P, D], F32) for i in range(VB)]
        vp = sb("vp", [P, 3, NKV], BF16)
        blk = [ctx.enter_context(nc.psum_tensor(f"proj_blk{i}", [P, D], F32)) for i in range(3)]
        tq = [ctx.enter_context(nc.psum_tensor(f"proj_tq{i}", [P, D], F32)) for i in range(2)]
        xp = ctx.enter_context(nc.psum_tensor("proj_xp", [P, 2 * D], F16))

        xin = [sem(f"xin{i}") for i in range(2)]
        xchain, scaled, xhigh, xlow, xturned, xt_done = (sem(s) for s in (
            "xchain", "x_scaled", "x_high", "x_low", "x_turned", "xt"))
        blk_done, blk_free, ss_done, chain, rooted, inv_done = (sem(s) for s in (
            "block", "block_read", "squares", "chain", "rooted", "inverse"))
        root_in = sem("mean")
        tab_done, ra_done, rb_done, tq_done, high, low = (sem(s) for s in (
            "tables", "first_product", "second_product", "heads_turned", "heads_high", "heads_low"))
        sum_done = [sem(f"rotated{i}") for i in range(2)]
        rn_done = [sem(f"normalised{i}") for i in range(2)]
        out_q = [sem(f"stored{i}") for i in range(2)]
        rest1, vmid, vlow, v_out = sem("v_rest"), sem("v_mid"), sem("v_low"), sem("v_stored")
        XSTEPS, CSTEPS, CHUNKS, TRIG = 7, 4, 6, 10
        angle, fold, turns = (raw[1][:, 2 * i:2 * i + 2, :].rearrange("p a d -> p (a d)").rearrange(
            "p (t c) -> p t c", c=HALF) for i in range(3))
        trig, waves = sem("angles"), sem("waves")
        craw = [sb(f"chunk{i}", [P, SC], F32) for i in range(3)]
        cparts = [sb(f"chunk_parts{i}", [P, 2 * SC], F16) for i in range(3)]
        c_in = [sem(f"chunk_in{i}") for i in range(3)]
        c_out = [sem(f"chunk_stored{i}") for i in range(3)]
        c_high, c_low = sem("chunk_high"), sem("chunk_low")

        def head_views(n):
            if n < QB:
                src = tq[n % 2][:, :].rearrange("p (h b s) -> p b h s", h=HB, b=BT)
                dst = turned[n % 2][:, :].rearrange("p (b two h s) -> p b two h s", b=BT, two=2, h=HB)
                return src, dst[:, :, 0], dst[:, :, 1]
            src = tq[n % 2][:, :].rearrange("p (h b s) -> p b h s", h=HB, b=BT)
            dst = turned[n % 2][:, :].rearrange("p (b h two s) -> p b h two s", b=BT, two=2, h=HB)
            return src, dst[:, :, :, 0], dst[:, :, :, 1]

        block = ctx.enter_context(nc.Block())

        def tiles(engine, body):
            body(0, 0)
            body(1, 1)
            with engine.Fori(2, NT - 3, 2) as t:
                body(t, 0)
                body(t + 1, 1)
            body(NT - 2, 0)
            body(NT - 1, 1)

        halves = SC // (HK * PS)
        key_c = (k_t.rearrange("(c n) p m -> c p n m", n=2 * halves),
                 k_d.rearrange("(c n) p m -> c p n m", n=2 * halves))
        value_c = (v_rows.rearrange("(c p) (n m) -> c p n m", p=P, m=SC),
                   v_d.rearrange("(c p) (n m) -> c p n m", p=P, m=2 * SC))
        out_c = (wo_t.rearrange("(c n p) m -> c p n m", p=P, n=2),
                 wo_d.rearrange("p (c n) h m -> c p n (h m)", n=2))

        def chunk(i, t, c):
            kind, half = divmod(c, 2)
            n = halves if kind == 0 else 1
            return (key_c, value_c, out_c)[kind][i][ds(t, 1), :, half * n:(half + 1) * n].rearrange(
                "o p n m -> (o p) n m")

        def chunk_views(c):
            m = (PS, HD, D)[c // 2]
            a = craw[c % 3][:, :].rearrange("p (n m) -> p n m", m=m)
            b = cparts[c % 3][:, :].rearrange("p (n h m) -> p n h m", h=2, m=m)
            return a, b[:, :, 0, :], b[:, :, 1, :]

        def count(t, n):
            return t * (ROT // 2) + n // 2

        def is_tile(t, n):
            return isinstance(t, int) and t == n

        @block.sync
        def _(sp):
            for i in range(2):
                sp.dma_start(x3[i][:, :], x3_d[i]).then_inc(xin[i], 16)

            def store_heads(t, n):
                idx = t * ROT + n
                sp.wait_ge(high, idx + 1)
                sp.wait_ge(low, idx + 1)
                src = turned[n % 2][:, :]
                if n < QB:
                    dst = q_d[ds(t, 1), n].rearrange("o p b c -> (o p) b c")
                    src = src.rearrange("p (b c) -> p b c", b=BT)
                else:
                    w = PG // KB
                    dst = kn_d[ds(t * BT, BT), :, (n - QB) * w:(n - QB + 1) * w].rearrange("b p c -> p b c")
                    src = src.rearrange("p (b c) -> p b c", b=BT)
                sp.dma_start(dst, src).then_inc(out_q[n % 2], 16)

            def store_values(t):
                sp.wait_ge(vmid, (t + 1) * VB)
                sp.wait_ge(vlow, (t + 1) * VB)
                for r, part in enumerate((0, 1, 2, 0)):
                    sp.dma_start(vn_d[r, ds(t * P, P), :], vp[:, part, :]).then_inc(v_out, 16)

            def load_chunk(t, c):
                src = chunk(0, t, c)
                sp.dma_start(craw[c % 3][:, :].rearrange("p (n m) -> p n m", n=src.shape[1]), src
                             ).then_inc(c_in[c % 3], 16)

            def store_chunk(t, c):
                dst = chunk(1, t, c)
                sp.wait_ge(c_low, t * CHUNKS + c + 1)
                sp.dma_start(dst, cparts[c % 3][:, :].rearrange("p (n m) -> p n m", n=dst.shape[1])
                             ).then_inc(c_out[c % 3], 16)

            def chunks(t, c):
                if c:
                    store_chunk(t, c - 1)
                elif not is_tile(t, 0):
                    store_chunk(t - 1, CHUNKS - 1)
                if c + 2 < CHUNKS:
                    load_chunk(t, c + 2)
                elif not is_tile(t, NT - 1):
                    load_chunk(t + 1, c + 2 - CHUNKS)

            for c in range(2):
                load_chunk(0, c)

            def body(t, p):
                for n in range(BLK):
                    if n % 2 == 0:
                        chunks(t, n // 2)
                    if not is_tile(t, 0) and n < ROT:
                        store_heads(t - 1, n)
                        if n == 6:
                            store_values(t - 1)
                    if n == 4 and not is_tile(t, NT - 2) and not is_tile(t, NT - 1):
                        sp.wait_ge(xhigh, t + 1)
                        sp.wait_ge(xlow, t + 1)
                        sp.dma_start(x3[p][:, :], x3_d[ds(t + 2, 1)].rearrange("o p d -> (o p) d")
                                     ).then_inc(xin[p], 16)

            tiles(sp, body)
            store_chunk(NT - 1, CHUNKS - 1)
            for n in range(ROT):
                store_heads(NT - 1, n)
                if n == 6:
                    store_values(NT - 1)
            for i in range(2):
                sp.wait_ge(out_q[i], 16 * (NT * ROT // 2))
            sp.wait_ge(v_out, 16 * NT * 4)
            for i in range(3):
                sp.wait_ge(c_out[i], 16 * NT * CHUNKS // 3)

        @block.tensor
        def _(pe):
            mm = nc.tensor.matmul

            def turn_x(t, p):
                pe.wait_ge(xhigh, t + 1)
                pe.wait_ge(xlow, t + 1)
                after(pe, xt_done, t)
                for k in range(KD):
                    for h, part in enumerate((xh, xl)):
                        at = (2 * k + h) * P
                        last = nc.tensor.transpose(xp[:, at:at + P], part[:, k * P:(k + 1) * P], ident16[:, :])
                last.then_inc(xturned, 1)

            def turn_heads(t, n):
                idx = t * ROT + n
                pe.wait_ge(rn_done[n % 2], count(t, n) + 1)
                after(pe, high, idx - 1)
                after(pe, low, idx - 1)
                for h in range(HB):
                    last = nc.tensor.transpose(tq[n % 2][:, h * P:(h + 1) * P], rn[n % 2][:, h * P:(h + 1) * P],
                                               ident[:, :])
                last.then_inc(tq_done, 1)

            def body(t, p):
                pe.wait_ge(xt_done, t + 1)
                for n in range(BLK):
                    after(pe, blk_free, t * BLK + n - 2)
                    out = blk[n % 3][:, :]
                    cols = slice(n * D, (n + 1) * D)
                    for k in range(KD):
                        mm(out, xt[p][:, k, 0, :], wh[:, k, cols], start=(k == 0), stop=False)
                        mm(out, xt[p][:, k, 0, :], wl[:, k, cols], start=False, stop=False)
                        last = mm(out, xt[p][:, k, 1, :], wh[:, k, cols], start=False, stop=(k == KD - 1))
                    last.then_inc(blk_done, 1)
                    if not is_tile(t, 0) and 1 <= n <= ROT:
                        turn_heads(t - 1, n - 1)
                    if n == ROT and not is_tile(t, NT - 1):
                        turn_x(t + 1, 1 - p)

            turn_x(0, 0)
            tiles(pe, body)
            for n in range(ROT):
                turn_heads(NT - 1, n)

        @block.scalar
        def _(act):
            copy = lambda out, in_, **kw: nc.scalar.activation(out, in_, ACT.Copy, **kw)

            def x_high(t, p):
                act.wait_ge(scaled, t + 1)
                after(act, xturned, t)
                copy(xh[:, :], x3[p][:, :], scale=col[p][:, 2:3]).then_inc(xhigh, 1)

            def heads_high(t, n):
                idx = t * ROT + n
                act.wait_ge(tq_done, idx + 1)
                after(act, out_q[n % 2], (t * (ROT // 2) + n // 2) * 16)
                src, dst, _ = head_views(n)
                copy(dst, src).then_inc(high, 1)

            def normalise(t, p, n):
                act.wait_ge(sum_done[n % 2], count(t, n) + 1)
                act.wait_ge(inv_done, t + 1)
                after(act, tq_done, t * ROT + n - 1)
                for h in range(HB):
                    cols = slice(h * HD, (h + 1) * HD)
                    last = copy(rn[n % 2][:, cols], rb[n % 2][:, cols],
                                scale=inv[p][:, n * HB + h:n * HB + h + 1])
                last.then_inc(rn_done[n % 2], 1)

            def middle(t, j):
                act.wait_ge(rest1, t * VB + j + 1)
                copy(vp[:, 1, j * D:(j + 1) * D], v32[j][:, :]).then_inc(vmid, 1)

            def behind(t, p, n):
                if n >= 2:
                    heads_high(t, n - 2)
                if n < ROT and n % 2:
                    normalise(t, p, n)
                if n % 2 == 0 and 2 <= n <= 2 * VB:
                    middle(t, n // 2 - 1)

            def chunk_high(t, c):
                act.wait_ge(c_in[c % 3], t * (16 * CHUNKS // 3) + (c // 3 + 1) * 16)
                after(act, c_out[c % 3], t * (16 * CHUNKS // 3) + c // 3 * 16)
                a, h, _ = chunk_views(c)
                copy(h, a, scale=up[:, c // 2:c // 2 + 1]).then_inc(c_high, 1)

            def body(t, p):
                for n in range(BLK):
                    if n == BLK - 1:
                        act.wait_ge(root_in, t + 1)
                        nc.scalar.activation(ss[:, 2, :], ss[:, 1, :], ACT.Sqrt).then_inc(rooted, 1)
                    if not is_tile(t, 0):
                        behind(t - 1, 1 - p, n)
                    if n % 2 == 0:
                        chunk_high(t, n // 2)
                    act.wait_ge(blk_done, t * BLK + n + 1)
                    if is_tile(t, 0) and n == BLK - 1:
                        act.wait_ge(trig, TRIG)
                        nc.scalar.activation(sin[:, :, :], angle, ACT.Sin)
                        nc.scalar.activation(cos[:, :, :], fold, ACT.Sin).then_inc(waves, 1)
                    if is_tile(t, 1) and n == 0:
                        act.wait_ge(waves, 1)
                    if n < ROT:
                        after(act, sum_done[n % 2], count(t - 2, n) + 1)
                        copy(raw[p][:, n, :], blk[n % 3][:, :])
                        after(act, ss_done, t * ROT + n - 1)
                        nc.scalar.activation(sq[n % 2][:, :], blk[n % 3][:, :], ACT.Square).then_inc(blk_free, 1)
                    else:
                        j = n - ROT
                        after(act, v_out, t * 4 * 16)
                        after(act, vlow, t * VB)
                        copy(v32[j][:, :], blk[n % 3][:, :], scale=col[p][:, 6:7])
                        copy(vp[:, 0, j * D:(j + 1) * D], blk[n % 3][:, :], scale=col[p][:, 6:7]
                             ).then_inc(blk_free, 1)
                    if n == ROT - 2 and not is_tile(t, NT - 1):
                        x_high(t + 1, 1 - p)

            x_high(0, 0)
            tiles(act, body)
            for n in range(ROT + 2):
                behind(NT - 1, 1, n)

        @block.gpsimd
        def _(pool):
            g = nc.gpsimd

            def tables(t):
                if is_tile(t, 0):
                    pool.wait_ge(waves, 1)
                for i in range(2):
                    after(pool, sum_done[i], count(t, 0))
                for i in range(2):
                    for tab, trig, w in ((ta, cos, wa), (tb, sin, wb)):
                        last = g.tensor_tensor(tab[:, i, :].rearrange("p (h c) -> p h c", h=2),
                                               trig[:, ds(t, 1), :].to_broadcast([P, 2, HALF]),
                                               w[:, i, :].rearrange("p (h c) -> p h c", h=2), ALU.mult)
                last.then_inc(tab_done, 1)
                pool.wait_ge(tab_done, t + 1)

            def first_product(t, p, n):
                after(pool, sum_done[n % 2], count(t, n))
                pool.wait_ge(blk_free, t * BLK + n + 1)
                g.tensor_tensor(ra[n % 2][:, :].rearrange("p (h c) -> p h c", h=HB),
                                raw[p][:, n, :].rearrange("p (h c) -> p h c", h=HB),
                                ta[:, n // QB, :].unsqueeze(1).to_broadcast([P, HB, HD]), ALU.mult
                                ).then_inc(ra_done, 1)

            def add(t, n):
                pool.wait_ge(rb_done, t * ROT + n + 1)
                pool.wait_ge(ra_done, t * ROT + n + 1)
                g.tensor_tensor(rb[n % 2][:, :], rb[n % 2][:, :], ra[n % 2][:, :], ALU.add
                                ).then_inc(sum_done[n % 2], 1)

            def rest(t, j):
                pool.wait_ge(blk_free, t * BLK + ROT + j + 1)
                g.tensor_tensor(v32[j][:, :], v32[j][:, :], vp[:, 0, j * D:(j + 1) * D], ALU.subtract
                                ).then_inc(rest1, 1)

            def rest_low(t, j):
                pool.wait_ge(vmid, t * VB + j + 1)
                g.tensor_tensor(vp[:, 2, j * D:(j + 1) * D], v32[j][:, :], vp[:, 1, j * D:(j + 1) * D],
                                ALU.subtract).then_inc(vlow, 1)

            def behind(t, p):
                for n in range(ROT):
                    first_product(t, p, n)
                    if n % 2 == 0:
                        add(t, n)
                    elif n < 2 * VB:
                        rest(t, n // 2)
                    elif n < 4 * VB:
                        rest_low(t, n // 2 - VB)

            def body(t, p):
                if not is_tile(t, 0):
                    behind(t - 1, 1 - p)
                tables(t)

            tiles(pool, body)
            behind(NT - 1, 1)

        @block.vector
        def _(dve):
            v = nc.vector

            def trig_step(n):
                if n:
                    dve.wait_ge(trig, n)
                per_tile = place[:, :].unsqueeze(2).to_broadcast([P, NT, HALF])
                per_pair = freq[:, :].unsqueeze(1).to_broadcast([P, NT, HALF])
                reduce = [lambda part=part: v.scalar_tensor_tensor(out=angle, in0=turns, scalar=-part, in1=angle,
                                                                   op0=ALU.mult, op1=ALU.add) for part in TWO_PI]
                ins = (
                    lambda: v.tensor_tensor(angle, per_tile, per_pair, ALU.mult),
                    lambda: v.tensor_scalar(out=turns, in0=angle, scalar1=1.0 / 6.283185307179586, scalar2=ROUND,
                                            op0=ALU.mult, op1=ALU.add),
                    lambda: v.tensor_scalar(out=turns, in0=turns, scalar1=-ROUND, scalar2=None, op0=ALU.add),
                    *reduce,
                    lambda: v.tensor_scalar(out=angle, in0=angle, scalar1=3.1415925, scalar2=-3.1415925, op0=ALU.min,
                                            op1=ALU.max),
                    lambda: v.tensor_scalar(out=fold, in0=angle, scalar1=-1.0, scalar2=None, op0=ALU.mult),
                    lambda: v.tensor_tensor(fold, fold, angle, ALU.min),
                    lambda: v.tensor_scalar(out=fold, in0=fold, scalar1=1.5707963267948966, scalar2=None,
                                            op0=ALU.add),
                )
                assert len(ins) == TRIG
                ins[n]().then_inc(trig, 1)

            def scale_step(t, p, n):
                c = col[p]
                if n:
                    dve.wait_ge(xchain, t * XSTEPS + n)
                else:
                    dve.wait_ge(xin[p], 8 * t + 8 * (2 - p))
                ins = (
                    lambda: v.tensor_reduce(c[:, 0:1], x3[p][:, :], AX.X, ALU.max, apply_absolute_value=True),
                    lambda: v.tensor_scalar(out=c[:, 0:1], in0=c[:, 0:1], scalar1=TINY, scalar2=None, op0=ALU.max),
                    lambda: v.tensor_scalar(out=c[:, 1:2].bitcast(I32), in0=c[:, 0:1].bitcast(I32),
                                            scalar1=EXPONENT, scalar2=None, op0=ALU.bitwise_and),
                    lambda: v.reciprocal(c[:, 3:4], c[:, 1:2]),
                    lambda: v.tensor_scalar(out=c[:, 2:3], in0=c[:, 3:4], scalar1=TOP, scalar2=None, op0=ALU.mult),
                    lambda: v.tensor_scalar(out=c[:, 6:7], in0=c[:, 1:2], scalar1=1.0 / TOP, scalar2=vw[:, :],
                                            op0=ALU.mult, op1=ALU.mult),
                    lambda: v.tensor_tensor(c[:, 4:5], c[:, 2:3], up[:, 3:4], ALU.mult),
                    lambda: v.scalar_tensor_tensor(out=c[:, 5:6], in0=c[:, 4:5], scalar=EPS, in1=c[:, 4:5],
                                                   op0=ALU.mult, op1=ALU.mult),
                )[n]()
                ins.then_inc(xchain if n < XSTEPS else scaled, 1)

            def x_low(t, p):
                dve.wait_ge(xhigh, t + 1)
                after(dve, xturned, t)
                v.scalar_tensor_tensor(out=xl[:, :], in0=x3[p][:, :], scalar=col[p][:, 2:3], in1=xh[:, :],
                                       op0=ALU.mult, op1=ALU.subtract).then_inc(xlow, 1)

            def keep_xt(t, p):
                dve.wait_ge(xturned, t + 1)
                v.tensor_copy(xt[p][:, :, :, :].rearrange("p k h c -> p (k h c)"), xp[:, :]).then_inc(xt_done, 1)

            def squares(t, n):
                dve.wait_ge(blk_free, t * BLK + n + 1)
                v.tensor_reduce(ss[:, 0, n * HB:(n + 1) * HB], sq[n % 2][:, :].rearrange("p (h c) -> p h c", h=HB),
                                AX.X, ALU.add).then_inc(ss_done, 1)

            def mean(t, p):
                dve.wait_ge(ss_done, (t + 1) * ROT)
                v.tensor_scalar(out=ss[:, 1, :], in0=ss[:, 0, :], scalar1=1.0 / HD, scalar2=col[p][:, 5:6],
                                op0=ALU.mult, op1=ALU.add).then_inc(root_in, 1)

            def inverse(t, p):
                n = [0]

                def step(ins):
                    n[0] += 1
                    ins.then_inc(chain, 1)
                    dve.wait_ge(chain, t * CSTEPS + n[0])

                for i in range(2):
                    after(dve, rn_done[i], count(t - 1, 0))
                dve.wait_ge(rooted, t + 1)
                step(v.reciprocal(ss[:, 3, :], ss[:, 2, :]))
                step(v.tensor_tensor(ss[:, 2, :], ss[:, 3, :], ss[:, 1, :], ALU.mult))
                step(v.tensor_tensor(ss[:, 2, :], ss[:, 2, :], ss[:, 3, :], ALU.mult))
                step(v.tensor_scalar(out=ss[:, 2, :], in0=ss[:, 2, :], scalar1=-0.5, scalar2=1.5, op0=ALU.mult,
                                     op1=ALU.add))
                v.tensor_tensor(inv[p][:, :], ss[:, 2, :], ss[:, 3, :], ALU.mult).then_inc(inv_done, 1)
                dve.wait_ge(inv_done, t + 1)
                assert n[0] == CSTEPS

            def rotate(t, p, n):
                idx = t * ROT + n
                src = raw[p][:, n, :].rearrange("p (h two c) -> p h two c", h=HB, two=2)
                dst = rb[n % 2][:, :].rearrange("p (h two c) -> p h two c", h=HB, two=2)
                after(dve, rn_done[n % 2], count(t, n))
                for half in range(2):
                    table = tb[:, n // QB, half * HALF:(half + 1) * HALF].unsqueeze(1).to_broadcast([P, HB, HALF])
                    last = v.tensor_tensor(dst[:, :, half, :], src[:, :, 1 - half, :], table, ALU.mult)
                last.then_inc(rb_done, 1)

            def add(t, n):
                idx = t * ROT + n
                dve.wait_ge(rb_done, idx + 1)
                dve.wait_ge(ra_done, idx + 1)
                v.tensor_tensor(rb[n % 2][:, :], rb[n % 2][:, :], ra[n % 2][:, :], ALU.add).then_inc(sum_done[n % 2], 1)

            def normalise(t, p, n):
                dve.wait_ge(sum_done[n % 2], count(t, n) + 1)
                after(dve, tq_done, t * ROT + n - 1)
                v.tensor_tensor(rn[n % 2][:, :].rearrange("p (h c) -> p h c", h=HB),
                                rb[n % 2][:, :].rearrange("p (h c) -> p h c", h=HB),
                                inv[p][:, n * HB:(n + 1) * HB].unsqueeze(2).to_broadcast([P, HB, HD]), ALU.mult
                                ).then_inc(rn_done[n % 2], 1)

            def heads_low(t, n):
                dve.wait_ge(high, t * ROT + n + 1)
                src, hi, lo = head_views(n)
                v.tensor_tensor(lo, src, hi, ALU.subtract).then_inc(low, 1)

            def chunk_low(t, c):
                dve.wait_ge(c_high, t * CHUNKS + c + 1)
                a, h, lo = chunk_views(c)
                v.scalar_tensor_tensor(out=lo, in0=a, scalar=up[:, c // 2:c // 2 + 1], in1=h, op0=ALU.mult,
                                       op1=ALU.subtract).then_inc(c_low, 1)

            def body(t, p):
                if not is_tile(t, 0):
                    dve.wait_ge(tab_done, t)
                for n in range(BLK):
                    if not is_tile(t, 0):
                        if n < ROT:
                            rotate(t - 1, 1 - p, n)
                            if n % 2:
                                add(t - 1, n)
                        if n >= 2:
                            heads_low(t - 1, n - 2)
                        if n < ROT and n % 2 == 0:
                            normalise(t - 1, 1 - p, n)
                    if 1 <= n <= ROT:
                        squares(t, n - 1)
                    if is_tile(t, 0) and n < TRIG:
                        trig_step(n)
                    if n % 2 == 1:
                        chunk_low(t, n // 2)
                    if not is_tile(t, NT - 1):
                        if n <= XSTEPS:
                            scale_step(t + 1, 1 - p, n)
                        if n == ROT - 1:
                            x_low(t + 1, 1 - p)
                        if n == ROT:
                            keep_xt(t + 1, 1 - p)
                    if n == ROT:
                        mean(t, p)
                    if n == BLK - 1:
                        inverse(t, p)

            for n in range(XSTEPS + 1):
                scale_step(0, 0, n)
            x_low(0, 0)
            keep_xt(0, 0)
            tiles(dve, body)
            dve.wait_ge(tab_done, NT)
            for n in range(0, ROT + 2, 2):
                if n < ROT:
                    rotate(NT - 1, 1, n)
                    rotate(NT - 1, 1, n + 1)
                    add(NT - 1, n + 1)
                    normalise(NT - 1, 1, n)
                if n >= 2:
                    heads_low(NT - 1, n - 2)
                    heads_low(NT - 1, n - 1)


def attention(nc, ident, cs, oscale, v_idx, lens_f, pages, k_d, v_d, kn_d, vn_d, q_d, wo_d, x3_d, out_v):
    U = BT * HK
    QUAD = 4
    START = 1
    ctx = ExitStack()
    with ctx:
        def sb(name, shape, dt):
            return ctx.enter_context(nc.sbuf_tensor("att_" + name, shape, dt))

        def sem(name):
            return ctx.enter_context(nc.semaphore("att_" + name))

        page_row = sb("page_row", [1, B * NPP], I32)
        wo = sb("wo", [P, HQ, 2, D], F16)
        keys = [sb(f"keys{i}", [P, NPP + 1, HK, 2, PS], F16) for i in range(2)]
        values = [sb(f"values{i}", [P, LC, HK, 2, HD], F16) for i in range(2)]
        fresh = [sb(f"fresh{i}", [P, HK, HD], BF16) for i in range(2)]
        query = [sb(f"query{i}", [P, HK, 2, P], F16) for i in range(2)]
        idx = [sb(f"idx{i}", [P, LC], U32) for i in range(2)]
        iota = sb("iota", [P, L], F16)
        mask = [sb(f"mask{i}", [P, S + L + S], F32) for i in range(2)]
        prob = [sb(f"prob{i}", [P, LK], F32) for i in range(2)]
        norm = [sb(f"norm{i}", [P, L + P], F32) for i in range(2)]
        col = [sb(f"col{i}", [P, 4], F32) for i in range(2)]
        tph = [sb(f"tph{i}", [P, L + P], F16) for i in range(2)]
        tpl = [sb(f"tpl{i}", [P, L], F16) for i in range(2)]
        ot = [sb(f"ot{i}", [P, 2, HQ, P], BF16) for i in range(2)]
        of = sb("of", [P, D], F32)
        res = [sb(f"res{i}", [P, D], F32) for i in range(2)]
        iota_i = prob[0][:, 0:L].bitcast(I32)
        banks = ctx.enter_context(nc.psum_tensor("att_scores", [P, 3 * D], F32))
        sc = [banks[:, 0:LK], banks[:, 3 * D - LK:3 * D]]
        tr = [ctx.enter_context(nc.psum_tensor(f"att_tr{i}", [P, D], F32)) for i in range(2)]
        tr_new = ctx.enter_context(nc.psum_tensor("att_tr_new", [P, D], F32))
        o_ps = ctx.enter_context(nc.psum_tensor("att_o", [P, D], F32))
        y_ps = ctx.enter_context(nc.psum_tensor("att_y", [P, D], F32))

        pages_in = sem("pages_in")
        wo_in, iota_int, iota_done, unmasked = sem("wo_in"), sem("iota_int"), sem("iota"), sem("unmasked")
        kq_in = [sem(f"keys_in{i}") for i in range(2)]
        vc_in = [sem(f"values_in{i}") for i in range(2)]
        vn_in = [sem(f"fresh_in{i}") for i in range(2)]
        x_in = [sem(f"x_in{i}") for i in range(2)]
        stored = [sem(f"stored{i}") for i in range(2)]
        idx_done, idx_seen, qk_seen = sem("idx"), sem("idx_seen"), sem("scores_seen")
        mask_done, qk_done, max_done, nb_done, exp_done = (sem(s) for s in (
            "mask", "scores", "max", "neg_max", "exp"))
        inv_done, norm_done, new_done = (sem(s) for s in ("sum_inverse", "normalised", "new_normalised"))
        tr_done, th_done, tl_done, pv_done = (sem(s) for s in ("turned", "high", "low", "weighted"))
        o_kept, oh_done, ol_done, y_done, res_done = (sem(s) for s in (
            "out", "out_high", "out_low", "projected", "result"))
        def quad_of_step(do, t, i, p):
            k = (i - 7) // QUAD
            if k < 0:
                do(t - 1, k + U // QUAD, 1 - p)
            else:
                do(t, k, p)

        def quad_views(k, p):
            bi, half = divmod(k, HK // QUAD)
            heads = slice(half * QUAD * REP, (half + 1) * QUAD * REP)
            src = of[:, :].rearrange("p (h s) -> p h s", s=S)
            return src, [ot[p][:, a, heads, bi * S:(bi + 1) * S] for a in range(2)]

        block = ctx.enter_context(nc.Block())

        def groups(engine, body):
            body(0, 0, 0)
            body(1, 1, 1)
            with engine.Fori(2, NT - 1, 2) as t:
                body(t, 0, 2)
                body(t + 1, 1, 2)

        def cached(q):
            return (slice(0, L), slice(L, LK)) if q == 0 else (slice(S, LK), slice(0, S))

        def heads_of_step(i):
            n = U - START
            j = i - START
            return range(j * HQ // n, (j + 1) * HQ // n) if j >= 0 else range(0)

        @block.sync
        def _(sp):
            def load(t, bi):
                p = bi % 2
                b = t * BT + bi
                after(sp, qk_done, (b - 1) * HK)
                sp.dma_start(keys[p][:, NPP].rearrange("p h two s -> p (h two s)"),
                             kn_d[ds(b, 1)].rearrange("o p m -> (o p) m")).then_inc(kq_in[p], 16)
                sp.dma_start(query[p][:, :, :, :].rearrange("p h two c -> p h (two c)"),
                             q_d[ds(t, 1), :, :, bi, :].rearrange("o g p c -> p (o g) c")).then_inc(kq_in[p], 16)
                if isinstance(b, int) and b == 0:
                    sp.wait_ge(pages_in, 16)
                for half in range(2):
                    _, pages = nc.values_load_multi_w_load_instructions(
                        page_row[0:1, ds(b * NPP + half * (NPP // 2), NPP // 2)], engines=(SP,), min_val=0,
                        max_val=PAGES - 1, skip_runtime_bounds_check_because="page numbers are below PAGES")
                    for j, page in enumerate(pages):
                        sp.dma_start(keys[p][:, half * (NPP // 2) + j].rearrange("p h two s -> p (h two s)"),
                                     k_d[ds(page, 1)].rearrange("o p m -> (o p) m")).then_inc(kq_in[p], 16)
                after(sp, pv_done, (b - 1) * HK)
                for r in range(BT):
                    sp.dma_start(fresh[p][r * S:(r + 1) * S, :, :].rearrange("p h c -> p (h c)"),
                                 vn_d[r, ds(b * S, S), :]).then_inc(vn_in[p], 16)

            def result(t, p):
                sp.wait_ge(res_done, t + 1)
                sp.dma_start(out_v[ds(t, 1)].rearrange("o p d -> (o p) d"), res[p][:, :]).then_inc(stored[p], 16)

            def body(t, p, past):
                for bi in range(BT):
                    load(t, bi)
                    if past == 0:
                        heads = slice(bi * (HQ // BT), (bi + 1) * (HQ // BT))
                        sp.dma_start(wo[:, heads, :, :], wo_d[:, heads, :, :]).then_inc(wo_in, 16)
                    if bi == 1 and past == 2:
                        result(t - 2, p)
                after(sp, stored[p], 8 * t - 8 * p)
                sp.dma_start(res[p][:, :], x3_d[ds(t, 1)].rearrange("o p d -> (o p) d")).then_inc(x_in[p], 16)

            sp.dma_start(page_row[:, :], pages.rearrange("(o b) j -> o (b j)", o=1)).then_inc(pages_in, 16)
            groups(sp, body)
            result(NT - 2, 0)
            result(NT - 1, 1)
            for p in range(2):
                sp.wait_ge(stored[p], 16 * (NT // 2))

        @block.gpsimd
        def _(pool):
            g = nc.gpsimd
            def gather(b, p, c):
                if c == 0:
                    after(pool, pv_done, (b - 1) * HK)
                    g.tensor_copy(idx[p][:, :], v_idx[:, ds(b * LC, LC)]).then_inc(idx_done, 1)
                    hold(pool, idx_done, b + 1, idx_seen)
                g.indirect_dma_start(out=values[p][:, c].rearrange("p h two d -> p (h two d)"),
                                     out_offset=None, in_=v_d,
                                     in_offset=bass.IndirectOffsetOnAxis(idx[p][:, c:c + 1], 0)
                                     ).then_inc(vc_in[p], 16)

            def new_tokens(n, q):
                pool.wait_ge(inv_done, n + 1)
                after(pool, tr_done, n - 1)
                g.tensor_tensor(norm[q][:, L:L + P].rearrange("p (a s) -> p a s", s=S),
                                prob[q][:, cached(q)[1]].unsqueeze(1).to_broadcast([P, 4, S]),
                                col[q][:, 3:4].unsqueeze(1).to_broadcast([P, 4, S]), ALU.mult
                                ).then_inc(new_done, 1)

            def out_low(t, k, p):
                pool.wait_ge(oh_done, t * (U // QUAD) + k + 1)
                src, dst = quad_views(k, p)
                g.tensor_tensor(dst[1], src, dst[0], ALU.subtract).then_inc(ol_done, 1)

            def body(t, p, past):
                for i in range(U):
                    if past or i:
                        new_tokens(t * U + i - 1, (i - 1) % 2)
                    if i % QUAD == 3 and (past or i > 3):
                        quad_of_step(out_low, t, i, p)
                    bi, c = i // HK + 1, i % HK - (HK - LC)
                    if c >= 0 and (bi < BT or not (isinstance(t, int) and t == NT - 1)):
                        gather(t * BT + bi, bi % 2, c)

            for c in range(LC):
                gather(0, 0, c)
            g.iota(iota_i, pattern=[[1, L]], base=0, channel_multiplier=0).then_inc(iota_int, 1)
            pool.wait_ge(iota_int, 1)
            g.tensor_copy(iota[:, :], iota_i).then_inc(iota_done, 1)
            body(0, 0, 0)
            body(1, 1, 1)
            with pool.Fori(2, NT - 3, 2) as t:
                body(t, 0, 2)
                body(t + 1, 1, 2)
            body(NT - 2, 0, 2)
            body(NT - 1, 1, 2)
            new_tokens(NT * U - 1, 1)
            out_low(NT - 1, U // QUAD - 1, 1)

        @block.tensor
        def _(pe):
            mm = nc.tensor.matmul

            def scores(t, i):
                bi, h = divmod(i, HK)
                p, q = bi % 2, i % 2
                n = t * U + i
                if h == 0:
                    pe.wait_ge(kq_in[p], (NPP + 2) * 16 * (t * (BT // 2) + bi // 2 + 1))
                after(pe, max_done, n)
                qh, ql = query[p][:, h, 0, :], query[p][:, h, 1, :]
                kh, kl = keys[p][:, 0:NPP, h, 0, :], keys[p][:, 0:NPP, h, 1, :]
                nh, nl = keys[p][:, NPP, h, 0, :], keys[p][:, NPP, h, 1, :]
                old, new = (sc[q][:, part] for part in cached(q))
                old = old.rearrange("p (n s) -> p n s", s=PS)
                for a, k, kn, start, stop in ((qh, kh, nh, True, False), (qh, kl, nl, False, False),
                                              (ql, kh, nh, False, True)):
                    mm(old, a, k, start=start, stop=stop)
                    last = mm(new, a, kn, start=start, stop=stop)
                last.then_inc(qk_done, 1)

            def turn(n, q):
                pe.wait_ge(norm_done, n + 1)
                after(pe, tl_done, n - 1)
                for c in range(LC):
                    nc.tensor.transpose(tr[q][:, c * P:(c + 1) * P], norm[q][:, c * P:(c + 1) * P], ident[:, :])
                pe.wait_ge(new_done, n + 1)
                after(pe, tl_done, n)
                nc.tensor.transpose(tr_new[:, 0:P], norm[q][:, L:L + P], ident[:, :]).then_inc(tr_done, 1)

            def weigh(t, i):
                bi, h = divmod(i, HK)
                p, q = bi % 2, i % 2
                n = t * U + i
                if h == 0:
                    pe.wait_ge(vc_in[p], LC * 16 * (t * (BT // 2) + bi // 2 + 1))
                    pe.wait_ge(vn_in[p], BT * 16 * (t * (BT // 2) + bi // 2 + 1))
                pe.wait_ge(tl_done, n + 1)
                if i % QUAD == 0:
                    after(pe, o_kept, t * (U // QUAD) + i // QUAD)
                out = o_ps[:, (i % QUAD) * P:(i % QUAD + 1) * P]
                for c in range(LC):
                    vh, vl = values[p][:, c, h, 0, :], values[p][:, c, h, 1, :]
                    th, tl = tph[q][:, c * P:(c + 1) * P], tpl[q][:, c * P:(c + 1) * P]
                    mm(out, vh, th, start=(c == 0), stop=False)
                    mm(out, vh, tl, start=False, stop=False)
                    mm(out, vl, th, start=False, stop=False)
                mm(out, fresh[p][:, h, :], tph[q][:, L:L + P], start=False, stop=True).then_inc(pv_done, 1)

            def project(t, p, h):
                if h == 0:
                    after(pe, res_done, t)
                if h == 0 or h == HQ // 2:
                    pe.wait_ge(ol_done, (t + 1) * (U // QUAD) - (1 if h == 0 else 0))
                for a, w, start, stop in ((0, 0, True, False), (0, 1, False, False), (1, 0, False, True)):
                    last = mm(y_ps[:, :], ot[p][:, a, h, :], wo[:, h, w, :], start=(h == 0 and start),
                              stop=(h == HQ - 1 and stop))
                if h == HQ - 1:
                    last.then_inc(y_done, 1)

            def body(t, p, past):
                for i in range(U):
                    scores(t, i)
                    if past or i >= 2:
                        turn(t * U + i - 2, i % 2)
                    if past:
                        if past == 1 and i == START:
                            pe.wait_ge(wo_in, BT * 16)
                        for h in heads_of_step(i):
                            project(t - 1, 1 - p, h)
                    if past or i >= 3:
                        weigh(*((t, i - 3) if i >= 3 else (t - 1, i - 3 + U)))

            groups(pe, body)
            for i in (U, U + 1):
                turn((NT - 1) * U + i - 2, i % 2)
                weigh(NT - 1, i - 3)
            weigh(NT - 1, U - 1)
            for h in range(HQ):
                project(NT - 1, (NT - 1) % 2, h)

        @block.scalar
        def _(act):
            copy = lambda out, in_, **kw: nc.scalar.activation(out, in_, ACT.Copy, **kw)

            def exps(n, q):
                act.wait_ge(nb_done, n + 1)
                nc.scalar.activation(prob[q][:, :], prob[q][:, :], ACT.Exp, bias=col[q][:, 1:2],
                                     scale=cs[:, 0:1], accum_out=col[q][:, 2:3]).then_inc(exp_done, 1)

            def high(n, q):
                act.wait_ge(tr_done, n + 1)
                after(act, pv_done, n - 1)
                copy(tph[q][:, 0:L], tr[q][:, :], scale=TOP)
                copy(tph[q][:, L:L + P], tr_new[:, 0:P], scale=TOP).then_inc(th_done, 1)

            def keep_out(t, k, p):
                act.wait_ge(pv_done, t * U + (k + 1) * QUAD)
                after(act, ol_done, t * (U // QUAD) + k)
                copy(of[:, :], o_ps[:, :], scale=1.0 / TOP).then_inc(o_kept, 1)

            def body(t, p, past):
                for i in range(U):
                    n = t * U + i
                    if i % QUAD == 3 and (past or i > 3):
                        quad_of_step(keep_out, t, i, p)
                    if past or i >= 2:
                        high(n - 2, i % 2)
                    exps(n, i % 2)

            groups(act, body)
            n = NT * U
            high(n - 2, 0)
            high(n - 1, 1)
            keep_out(NT - 1, U // QUAD - 1, 1)

        @block.vector
        def _(dve):
            v = nc.vector

            def make_mask(t, bi):
                b = t * BT + bi
                v.tensor_scalar(out=mask[bi % 2][:, S:S + L], in0=iota[:, :], scalar1=lens_f[:, ds(b, 1)],
                                scalar2=MASKED, op0=ALU.is_ge, op1=ALU.mult).then_inc(mask_done, 1)

            def maximum(t, i):
                bi, h = divmod(i, HK)
                q = i % 2
                n = t * U + i
                if h == 0:
                    make_mask(t, bi)
                    dve.wait_ge(mask_done, t * BT + bi + 1)
                after(dve, norm_done, n - 1)
                after(dve, new_done, n - 1)
                hold(dve, qk_done, n + 1, qk_seen)
                at = S if q == 0 else 0
                v.tensor_tensor_reduce(out=prob[q][:, :], in0=sc[q], in1=mask[bi % 2][:, at:at + LK], scale=1.0,
                                       scalar=-3.0e38, op0=ALU.add, op1=ALU.max, accum_out=col[q][:, 0:1]
                                       ).then_inc(max_done, 1)

            def negative(n, q):
                dve.wait_ge(max_done, n + 1)
                v.tensor_scalar(out=col[q][:, 1:2], in0=col[q][:, 0:1], scalar1=cs[:, 1:2], scalar2=None,
                                op0=ALU.mult).then_inc(nb_done, 1)

            def inverse(n, q):
                dve.wait_ge(exp_done, n + 1)
                v.reciprocal(col[q][:, 3:4], col[q][:, 2:3]).then_inc(inv_done, 1)

            def normalise(n, q):
                dve.wait_ge(inv_done, n + 1)
                after(dve, tr_done, n - 1)
                v.tensor_scalar(out=norm[q][:, 0:L], in0=prob[q][:, cached(q)[0]], scalar1=col[q][:, 3:4],
                                scalar2=None, op0=ALU.mult).then_inc(norm_done, 1)

            def low(n, q):
                dve.wait_ge(th_done, n + 1)
                after(dve, pv_done, n - 1)
                v.scalar_tensor_tensor(out=tpl[q][:, :], in0=tr[q][:, :], scalar=TOP, in1=tph[q][:, 0:L],
                                       op0=ALU.mult, op1=ALU.subtract)
                rows = slice(3 * S, 4 * S)
                v.scalar_tensor_tensor(out=tph[q][rows, L:L + P], in0=tr_new[rows, 0:P], scalar=TOP,
                                       in1=tph[q][rows, L:L + P], op0=ALU.mult, op1=ALU.subtract
                                       ).then_inc(tl_done, 1)

            def out_high(t, k, p):
                dve.wait_ge(o_kept, t * (U // QUAD) + k + 1)
                if k == 0:
                    after(dve, y_done, t - 1)
                src, dst = quad_views(k, p)
                v.tensor_copy(dst[0], src).then_inc(oh_done, 1)

            def result(t, p):
                dve.wait_ge(y_done, t + 1)
                dve.wait_ge(x_in[p], 8 * t + 8 * (2 - p))
                v.scalar_tensor_tensor(out=res[p][:, :], in0=y_ps[:, :], scalar=oscale[:, :], in1=res[p][:, :],
                                       op0=ALU.mult, op1=ALU.add).then_inc(res_done, 1)

            def body(t, p, past):
                for i in range(U):
                    n = t * U + i
                    maximum(t, i)
                    if past or i >= 1:
                        inverse(n - 1, (i - 1) % 2)
                    negative(n, i % 2)
                    if past or i >= 1:
                        normalise(n - 1, (i - 1) % 2)
                    if past or i >= 2:
                        low(n - 2, i % 2)
                    if i == 0 and past == 2:
                        result(t - 2, p)
                    if i % QUAD == 3 and (past or i > 3):
                        quad_of_step(out_high, t, i, p)

            v.memset(mask[0][:, :], 0.0).then_inc(unmasked, 1)
            v.memset(mask[1][:, :], 0.0).then_inc(unmasked, 1)
            dve.wait_ge(unmasked, 2)
            dve.wait_ge(iota_done, 1)
            groups(dve, body)
            n = NT * U
            inverse(n - 1, 1)
            normalise(n - 1, 1)
            low(n - 2, 0)
            result(NT - 2, 0)
            low(n - 1, 1)
            out_high(NT - 1, U // QUAD - 1, 1)
            result(NT - 1, 1)


def kernel(x, itok_B_0_15, itok_B_0_7, itok_Bx16_0_63, itok_B_207_1644, L0_cond_weights, L1_cond_W, L1_cond_Wr,
           L1_cond_A, L1_cond_B, L2_cond_weights, L3_cond_Wq, L3_cond_Wk, L3_cond_Wv, L3_cond_Wo,
           L3_cond_q_norm_w, L3_cond_k_norm_w, L3_cond_k_cache, L3_cond_v_cache):
    import numpy as np
    import concourse.bacc as bacc
    from concourse.bass_utils import run_bass_kernel_spmd

    def per_group(a):
        return np.asarray(a).reshape(NT, BT).T

    power = np.float32(10000.0) ** (np.arange(0, HD, 2, dtype=np.float32) / np.float32(HD))
    laid_out = [
        ("x", x),
        ("per_row", np.concatenate([per_group(itok_B_0_15), per_group(itok_B_0_7), per_group(itok_B_207_1644),
                                    np.asarray(itok_Bx16_0_63).reshape(B * LC, BT).T], axis=1)),
        ("lens", itok_B_207_1644),
        ("pages", itok_Bx16_0_63),
        ("mixers", np.concatenate([np.asarray(w).reshape(SETS * S, MIX) for w in (L0_cond_weights, L2_cond_weights)],
                                  axis=1)),
        ("lin_t", np.asarray(L1_cond_W).T),
        ("route_t", np.concatenate([np.asarray(L1_cond_Wr), np.asarray(L1_cond_A).reshape(ER, D)]).T),
        ("b_t", np.asarray(L1_cond_B).transpose(0, 2, 1).reshape(ER, D)),
        ("w_t", np.concatenate([np.asarray(w) for w in (L3_cond_Wq, L3_cond_Wk, L3_cond_Wv)]).T),
        ("wo_t", np.asarray(L3_cond_Wo).T),
        ("q_norm", L3_cond_q_norm_w),
        ("k_norm", L3_cond_k_norm_w),
        ("k_t", np.asarray(L3_cond_k_cache).transpose(0, 3, 2, 1).reshape(PAGES, P, HK * PS)),
        ("v_rows", np.asarray(L3_cond_v_cache).reshape(PAGES * PS, NKV)),
        ("inv_freq", (np.float32(1.0) / power).astype(np.float32)),
    ]
    nc = bacc.Bacc("TRN2", target_bir_lowering=False, num_devices=1)
    arrays, args = {}, []
    for name, a in laid_out:
        a = np.ascontiguousarray(a)
        arrays["in_" + name] = a
        args.append(nc.dram_tensor("in_" + name, a.shape, mybir.dt.from_np(a.dtype), kind="ExternalInput").ap())
    args.append(nc.dram_tensor("out_0", (B, S, D), F32, kind="ExternalOutput").ap())
    conditional_residual(nc, *args)
    got = run_bass_kernel_spmd(nc, [arrays], core_ids=[0])
    return got.results[0]["out_0"]
```
